# Optimizing a Trainium2 kernel written in Bass

```python
import numpy as np
import jax
import jax.numpy as jnp

def _softmax(x, axis=-1):
    return jax.nn.softmax(x, axis=axis)

def _gelu(x):
    return jax.nn.gelu(x, approximate=True)

def _silu(x):
    return jax.nn.silu(x)

def _sigmoid(x):
    return jax.nn.sigmoid(x)

def _layernorm(x, axis=-1, eps=1e-05):
    m = jnp.mean(x, axis=axis, keepdims=True)
    v = jnp.var(x, axis=axis, keepdims=True)
    return (x - m) / jnp.sqrt(v + eps)

def _scatter_add(tgt, idx, src, axis=0):
    return tgt.at[idx].add(src)

def _segment_sum(src, seg, n):
    return jax.ops.segment_sum(src, seg, n)
kernel_name = 'mk_adaln_d1_jaxref_r8_123a10'

def setup_inputs(seed: int=0):
    np.random.seed(seed)
    _w = jnp.asarray

    def _L0_attn_setup():
        import jax, jax.numpy as jnp
        import numpy as np
        N_HEAD = 16
        PAGE_SIZE = 32
        ROPE_THETA = 10000.0

        def _rope_tables(T, D, dtype):
            inv = 1.0 / ROPE_THETA ** (np.arange(0, D, 2, dtype=np.float32) / D)
            ang = np.outer(np.arange(T, dtype=np.float32), inv)
            return (jnp.asarray(np.cos(ang), dtype), jnp.asarray(np.sin(ang), dtype))

        def _apply_rope(x, cos, sin):
            x1 = x[..., 0::2]
            x2 = x[..., 1::2]
            c = cos[None, :, None, :]
            s = sin[None, :, None, :]
            out = jnp.stack([x1 * c - x2 * s, x1 * s + x2 * c], axis=-1)
            return out.reshape(x.shape)
        key = jax.random.key(seed)
        ks = jax.random.split(key, 6)
        B, T, E = (2, 256, 128)
        L = E // 2
        sc = lambda fan: 1.0 / np.sqrt(fan)
        return {'x': jax.random.normal(ks[0], (B, T, E), jnp.float32), 'wq': jax.random.normal(ks[1], (E, E), jnp.float32) * sc(E), 'w_down': jax.random.normal(ks[2], (E, L), jnp.float32) * sc(E), 'wk_up': jax.random.normal(ks[3], (L, E), jnp.float32) * sc(L), 'wv_up': jax.random.normal(ks[4], (L, E), jnp.float32) * sc(L), 'wo': jax.random.normal(ks[5], (E, E), jnp.float32) * sc(E)}
    _L0_attn_in = _L0_attn_setup()

    def _L0_ffn_setup():
        import jax, jax.numpy as jnp
        import numpy as np
        B, S, H, F, E, R, TOPK = (4, 256, 128, 512, 4, 4, 2)

        def _more_forward(x, Wg, bg, W1, b1, W2, b2):
            b, s, h = x.shape
            cur = x
            for r in range(R):
                flat = cur.reshape(-1, h)
                logits = flat @ Wg[r] + bg[r]
                vals, idx = jax.lax.top_k(logits, TOPK)
                w = jax.nn.softmax(vals, axis=-1)
                cw = jnp.sum(jax.nn.one_hot(idx, E, dtype=flat.dtype) * w[..., None], axis=1)
                hmid = jax.nn.gelu(jnp.einsum('nh,ehf->enf', flat, W1) + b1[:, None, :])
                y = jnp.einsum('enf,efh->enh', hmid, W2) + b2[:, None, :]
                out = jnp.einsum('ne,enh->nh', cw, y)
                cur = cur + out.reshape(b, s, h)
            return cur
        key = jax.random.key(seed)
        ks = jax.random.split(key, 8)
        scale = 0.02
        return {'x': jax.random.normal(ks[0], (B, S, H), dtype=jnp.float32), 'Wg': jax.random.normal(ks[1], (R, H, E), dtype=jnp.float32) * scale, 'bg': jnp.zeros((R, E), dtype=jnp.float32), 'W1': jax.random.normal(ks[2], (E, H, F), dtype=jnp.float32) * scale, 'b1': jnp.zeros((E, F), dtype=jnp.float32), 'W2': jax.random.normal(ks[3], (E, F, H), dtype=jnp.float32) * scale, 'b2': jnp.zeros((E, H), dtype=jnp.float32)}
    _L0_ffn_in = _L0_ffn_setup()
    _L0_c = _w((lambda *s: np.random.randn(*s).astype(np.float32) * 0.05)(2, 128))
    _L0_wmod = _w((lambda *s: np.random.randn(*s).astype(np.float32) * 0.05)(128, 6 * 128) * 128 ** (-0.5))
    _d = {'L0_attn_x': _L0_attn_in['x'], 'L0_attn_wq': _L0_attn_in['wq'], 'L0_attn_w_down': _L0_attn_in['w_down'], 'L0_attn_wk_up': _L0_attn_in['wk_up'], 'L0_attn_wv_up': _L0_attn_in['wv_up'], 'L0_attn_wo': _L0_attn_in['wo'], 'L0_ffn_Wg': _L0_ffn_in['Wg'], 'L0_ffn_bg': _L0_ffn_in['bg'], 'L0_ffn_W1': _L0_ffn_in['W1'], 'L0_ffn_b1': _L0_ffn_in['b1'], 'L0_ffn_W2': _L0_ffn_in['W2'], 'L0_ffn_b2': _L0_ffn_in['b2'], 'L0_c': _L0_c, 'L0_wmod': _L0_wmod}
    _x0 = _d['L0_attn_x']
    _d['L0_attn_x'] = jax.random.normal(jax.random.fold_in(jax.random.key(seed), 1), (2, 1024, 128), dtype=_x0.dtype)
    del _x0
    return _d

def reference(L0_attn_x, L0_attn_wq, L0_attn_w_down, L0_attn_wk_up, L0_attn_wv_up, L0_attn_wo, L0_ffn_Wg, L0_ffn_bg, L0_ffn_W1, L0_ffn_b1, L0_ffn_W2, L0_ffn_b2, L0_c, L0_wmod):

    def _L0_attn_ref(x, wq, w_down, wk_up, wv_up, wo):
        import jax, jax.numpy as jnp
        import numpy as np
        N_HEAD = 16
        PAGE_SIZE = 32
        ROPE_THETA = 10000.0

        def _rope_tables(T, D, dtype):
            inv = 1.0 / ROPE_THETA ** (np.arange(0, D, 2, dtype=np.float32) / D)
            ang = np.outer(np.arange(T, dtype=np.float32), inv)
            return (jnp.asarray(np.cos(ang), dtype), jnp.asarray(np.sin(ang), dtype))

        def _apply_rope(x, cos, sin):
            x1 = x[..., 0::2]
            x2 = x[..., 1::2]
            c = cos[None, :, None, :]
            s = sin[None, :, None, :]
            out = jnp.stack([x1 * c - x2 * s, x1 * s + x2 * c], axis=-1)
            return out.reshape(x.shape)
        B, T, E = x.shape
        H = N_HEAD
        D = E // H
        q = (x @ wq).reshape(B, T, H, D)
        lat = x @ w_down
        k = (lat @ wk_up).reshape(B, T, H, D)
        v = (lat @ wv_up).reshape(B, T, H, D)
        cos, sin = _rope_tables(T, D, x.dtype)
        q = _apply_rope(q, cos, sin)
        k = _apply_rope(k, cos, sin)
        scale = 1.0 / jnp.sqrt(jnp.asarray(D, x.dtype))
        scores = jnp.einsum('bqhd,bkhd->bhqk', q, k) * scale
        pages = jnp.arange(T) // PAGE_SIZE
        allowed = pages[None, :] <= pages[:, None]
        scores = jnp.where(allowed[None, None], scores, jnp.finfo(scores.dtype).min)
        attn = jax.nn.softmax(scores, axis=-1)
        out = jnp.einsum('bhqk,bkhd->bqhd', attn, v).reshape(B, T, E)
        return out @ wo

    def _L0_ffn_ref(x, Wg, bg, W1, b1, W2, b2):
        import jax, jax.numpy as jnp
        import numpy as np
        B, S, H, F, E, R, TOPK = (4, 256, 128, 512, 4, 4, 2)

        def _more_forward(x, Wg, bg, W1, b1, W2, b2):
            b, s, h = x.shape
            cur = x
            for r in range(R):
                flat = cur.reshape(-1, h)
                logits = flat @ Wg[r] + bg[r]
                vals, idx = jax.lax.top_k(logits, TOPK)
                w = jax.nn.softmax(vals, axis=-1)
                cw = jnp.sum(jax.nn.one_hot(idx, E, dtype=flat.dtype) * w[..., None], axis=1)
                hmid = jax.nn.gelu(jnp.einsum('nh,ehf->enf', flat, W1) + b1[:, None, :])
                y = jnp.einsum('enf,efh->enh', hmid, W2) + b2[:, None, :]
                out = jnp.einsum('ne,enh->nh', cw, y)
                cur = cur + out.reshape(b, s, h)
            return cur
        return _more_forward(x, Wg, bg, W1, b1, W2, b2)
    x = L0_attn_x
    mod = (_silu(L0_c) @ L0_wmod).reshape(L0_c.shape[0], 6, 1, -1)
    sa, ca, ga, sb, cb, gb = (mod[:, 0], mod[:, 1], mod[:, 2], mod[:, 3], mod[:, 4], mod[:, 5])
    ga = (2 * (ga >= 0) - 1) * jnp.maximum(jnp.abs(ga), 0.25)
    gb = (2 * (gb >= 0) - 1) * jnp.maximum(jnp.abs(gb), 0.25)
    h = _layernorm(x, axis=-1) * (1 + ca) + sa
    x = x + ga * _L0_attn_ref(h, L0_attn_wq, L0_attn_w_down, L0_attn_wk_up, L0_attn_wv_up, L0_attn_wo)
    h = _layernorm(x, axis=-1) * (1 + cb) + sb
    x = x + gb * _L0_ffn_ref(h, L0_ffn_Wg, L0_ffn_bg, L0_ffn_W1, L0_ffn_b1, L0_ffn_W2, L0_ffn_b2)
    return x

_drawn_inputs = setup_inputs


def setup_inputs(seed=0):
    import zlib

    import numpy as np

    out = dict(_drawn_inputs(seed))
    spreads = {'L0_ffn_bg': (0.0, 0.484), 'L0_ffn_b1': (0.0, 0.625), 'L0_ffn_b2': (0.0, 0.1)}
    factors = {}
    for name, (base, spread) in spreads.items():
        noise = np.random.default_rng([zlib.crc32(name.encode()), seed]).standard_normal(out[name].shape)
        drawn = base * np.exp(spread * noise) if base else spread * noise
        out[name] = jnp.asarray(drawn.astype(out[name].dtype))
    for name, factor in factors.items():
        out[name] = (out[name] * factor).astype(out[name].dtype)
    return out
```

```python
import concourse.bass as bass
import numpy as np
from concourse import mybir
from contextlib import ExitStack

F32 = mybir.dt.float32
F32R = mybir.dt.float32r
BF16 = mybir.dt.bfloat16
ALU = mybir.AluOpType
ACT = mybir.ActivationFunctionType
AX = mybir.AxisListType

P = 128
B, T, E = 2, 1024, 128
NH, D = 16, 8
LAT = 64
NE, R, FF = 4, 4, 512
PAGE = 32
TOK = B * T
NT = TOK // P
CH = 512
NCH = TOK // CH
TPC = CH // P
JB = T // P
HG = 4
NG = NH // HG
GROUPS = B * NG
SLOTS = 3
SCALE = float(D) ** -0.5
EPS = 1e-5

Q_PIECE = [0, 0, 0, 1, 1, 2]
K_PIECE = [0, 1, 2, 0, 1, 0]
TERMS = len(Q_PIECE)
ROW_ZERO = TERMS * D
ROW_PAGE = 64
ROW_MAX = P - 3
NPAGE = T // PAGE
MASKED = -3.0e38

UNITS = [
    [(0, 0, 0, 0, 512)],
    [(1, 0, 0, 0, 512)],
    [(0, 2, 0, 256, 256), (1, 6, 256, 256, 256)],
    [(0, 1, 0, 128, 384), (0, 3, 384, 384, 128)],
    [(1, 1, 0, 0, 512)],
    [(1, 2, 0, 0, 512)],
    [(1, 3, 0, 0, 512)],
    [(1, 4, 0, 0, 512)],
    [(1, 5, 0, 128, 384), (1, 7, 384, 384, 128)],
]
NU = len(UNITS)
FIRST_UNIT = [0, 1]
LAST_UNIT = [3, NU - 1]

BINS = [
    ([(0, 0), (4, 512)], 128, 0, 8),
    ([(1, 0), (5, 512)], 256, 1, 8),
    ([(2, 0)], 384, 2, 1),
    ([(6, 512)], 384, 10, 1),
    ([(3, 0)], 512, 3, 1),
    ([(4, 0)], 512, 4, 1),
    ([(5, 0)], 512, 5, 1),
    ([(6, 0)], 512, 6, 1),
    ([(7, 0)], 512, 7, 1),
    ([(7, 512)], 512, 11, 1),
]
GROUP_BINS = [(h, n) for h in range(HG) for n in range(len(BINS))]
NB = len(GROUP_BINS) + 1
LEAD = 3
PARTS = [GROUP_BINS[u * (NB - 1) // NU:(u + 1) * (NB - 1) // NU] for u in range(NU)]
BEFORE = [u * (NB - 1) // NU for u in range(NU)]



class Mem:

    def __init__(self, nc, stack):
        self.nc, self.stack = nc, stack

    def sb(self, name, shape, dt=F32):
        return self.stack.enter_context(self.nc.sbuf_tensor(name, shape, dt))

    def ps(self, name, shape, dt=F32):
        return self.stack.enter_context(self.nc.psum_tensor(name, shape, dt))

    def sem(self, name):
        return self.stack.enter_context(self.nc.semaphore(name))


def adaln_block(nc, w, out):
    with ExitStack() as stack:
        m = Mem(nc, stack)
        m.w, m.out = w, out
        m.qp = nc.dram_tensor("q_pieces", (GROUPS, 3, HG * D, T), BF16).ap()
        m.kp = nc.dram_tensor("k_pieces", (GROUPS, 3, HG * D, T), BF16).ap()
        m.x = m.sb("x_sb", [P, NT, E])
        m.ident = m.sb("ident", [P, P])
        m.identb = m.sb("identb", [P, P], BF16)
        m.modc = m.sb("modc", [P, 6, B])
        m.gbd = m.sb("gb_diag", [P, B, P])
        m.wog = m.sb("wog", [P, B, E])
        m.w1_hi = m.sb("w1_hi", [P, NE, FF], F32R)
        m.w1_lo = m.sb("w1_lo", [P, NE, FF], F32R)
        m.w2_hi = m.sb("w2_hi", [P, NE * FF // P, E], F32R)
        m.w2_lo = m.sb("w2_lo", [P, NE * FF // P, E], F32R)
        m.cur = m.sb("cur", [P, NCH, CH])
        m.mv = m.sb("mv", [P, NT, 2])
        m.stats = m.sb("stats", [P, NT, 6])
        m.ve = m.sb("ve", [P, NT, 1])
        m.sd = m.sb("sd", [P, NT, 1])
        m.rstd = m.sb("rstd", [P, NT, 1])
        m.nw = m.sb("nw", [P, NT, 1])
        m.wg = m.sb("wg_sb", [P, R, NE])
        m.bg = m.sb("bg_sb", [P, R, 1, NE])
        m.b1 = m.sb("b1_sb", [P, NE, FF // P])
        m.b2 = m.sb("b2_sb", [P, NE])
        m.tri = m.sb("tri", [P, 2, NE, NE])
        with ExitStack() as upto_attention:
            ma = Mem(nc, upto_attention)
            m.v = ma.sb("v_all", [P, GROUPS, JB, HG * D])
            m.ks = [ma.sb(f"ks{s}", [P, HG, T], BF16) for s in range(SLOTS)]
            m.qs = [ma.sb(f"qs{s}", [P, HG, T], BF16) for s in range(SLOTS)]
            with ExitStack() as part:
                prep(nc, m, Mem(nc, part))
            m.ovs = ma.sb("ovs", [P, GROUPS, 2, CH])
            with ExitStack() as part:
                attention(nc, m, Mem(nc, part))
            with ExitStack() as part:
                project(nc, m, Mem(nc, part))
        with ExitStack() as part:
            ffn(nc, m, Mem(nc, part))


def rstd_steps(nc, v, link, var_ok, sqrt_ok, m):
    nc.vector.tensor_scalar(m.ve[:, :, :], m.mv[:, :, 1:2], EPS, None, ALU.add).then_inc(var_ok, 1)
    v.wait_ge(sqrt_ok, 1)
    link(nc.vector.reciprocal(m.rstd[:, :, :], m.sd[:, :, :]))
    link(nc.vector.tensor_tensor(m.nw[:, :, :], m.rstd[:, :, :], m.rstd[:, :, :], ALU.mult))
    link(nc.vector.tensor_tensor(m.nw[:, :, :], m.nw[:, :, :], m.ve[:, :, :], ALU.mult))
    link(nc.vector.tensor_scalar(m.nw[:, :, :], m.nw[:, :, :], -0.5, 1.5, ALU.mult, ALU.add))
    link(nc.vector.tensor_tensor(m.rstd[:, :, :], m.rstd[:, :, :], m.nw[:, :, :], ALU.mult))


def prep(nc, m, l):
    w = m.w
    ct, ce, sc = (l.sb(n, [P, B]) for n in ("ct", "ce", "sc"))
    wmod = l.sb("wmod", [P, 6 * E])
    wq, wqs = l.sb("wq", [E, E]), l.sb("wqs", [E, E])
    wd = l.sb("wd", [E, LAT])
    wk, wks = l.sb("wk", [LAT, E]), l.sb("wks", [LAT, E])
    wv = l.sb("wv", [LAT, E])
    wo = l.sb("wo", [E, E])
    cos, sin = l.sb("cos", [P, T]), l.sb("sin", [P, T])
    xn = l.sb("xn", [P, NT, E])
    lat = l.sb("lat", [LAT, 2, CH])
    ga = l.sb("ga", [P, B, E])
    gt, gs = l.sb("gt", [P, B, E]), l.sb("gs", [P, B, E])
    bt, bs = l.sb("bt", [P, B]), l.sb("bs", [P, B])
    rc = [l.sb(f"rc{s}", [P, CH]) for s in "qk"]
    rs = [l.sb(f"rs{s}", [P, CH]) for s in "qk"]
    ro = [l.sb(f"ro{s}", [P, CH]) for s in "qk"]
    rr = [l.sb(f"rr{s}", [P, CH]) for s in "qk"]
    pieces = [l.sb(f"pieces_{s}", [P, B, 3, T], BF16) for s in "qk"]
    turned = [l.ps(f"turned{i}", [P, CH]) for i in range(2)]
    pq = [l.ps(f"pq{i}", [P, CH]) for i in range(2)]
    pk = [l.ps(f"pk{i}", [P, CH]) for i in range(2)]
    plv = l.ps("plv", [P, CH])
    pmod = l.ps("pmod", [P, CH])

    in_mod, in_w, in_tab, in_rows = (l.sem(n) for n in ("in_mod", "in_w", "in_tab", "in_rows"))
    in_x = [l.sem(f"in_x{c}") for c in range(NCH)]
    exp_c, silu_c, mods, mod_read = (l.sem(n) for n in ("exp_c", "silu_c", "mods", "mod_read"))
    var_ok, sqrt_ok, xn_ok, turn_ok, h_ok = (l.sem(n) for n in ("var_ok", "sqrt_ok", "xn_ok", "turn_ok", "h_ok"))
    swap_ok, q_ok, lat_ok, lat_sb, k_ok, v_ok, v_sb = (
        l.sem(n) for n in ("swap_ok", "q_ok", "lat_ok", "lat_sb", "k_ok", "v_ok", "v_sb"))
    rot, rot_read = l.sem("rot"), l.sem("rot_read")
    piece0, piece1, piece2, rest = (l.sem(n) for n in ("piece0", "piece1", "piece2", "rest"))
    dve, zeroed, pieces_out = l.sem("dve_prep"), l.sem("zeroed"), l.sem("pieces_out")

    with nc.Block() as block:

        @block.sync
        def _(sp):
            x_dram = w["x"].rearrange("b (t p) e -> p (b t) e", p=P)
            for c in range(NCH):
                sp.dma_start(m.x[:, TPC * c:TPC * (c + 1), :], x_dram[:, TPC * c:TPC * (c + 1), :]).then_inc(in_x[c], 16)
            sp.dma_start(cos[:, :], w["cos"]).then_inc(in_tab, 16)
            sp.dma_start(sin[:, :], w["sin"]).then_inc(in_tab, 16)
            for s in range(SLOTS):
                for rows, dst in ((w["k_rows"].bitcast(BF16), m.ks[s]), (w["q_rows"].bitcast(BF16), m.qs[s])):
                    n = rows.shape[0]
                    for h in range(HG):
                        sp.dma_start(dst[ROW_ZERO:ROW_ZERO + n, h, :], rows).then_inc(in_rows, 16)
            for b in range(B):
                sp.wait_ge(piece0, 4 * (b + 1))
                sp.wait_ge(piece1, 4 * (b + 1))
                sp.wait_ge(piece2, 4 * (b + 1))
                for side, dst in enumerate((m.qp, m.kp)):
                    for hg in range(NG):
                        sp.dma_start(dst[b * NG + hg].rearrange("c r t -> r c t"),
                                     pieces[side][32 * hg:32 * hg + 32, b, :, :]).then_inc(pieces_out, 16)
            sp.wait_ge(in_rows, 16 * SLOTS * HG * 2)
            sp.wait_ge(pieces_out, 16 * B * NG * 2)

        @block.scalar
        def _(act):
            act.dma_start(ct[:, :], w["c"]).then_inc(in_mod, 16)
            act.dma_start(wmod[:, :], w["wmod"]).then_inc(in_mod, 16)
            act.dma_start(m.ident[:, :], w["ident"]).then_inc(in_mod, 16)
            for dst, name in ((wq, "wq"), (wd, "w_down"), (wk, "wk_up"), (wv, "wv_up"), (wo, "wo")):
                act.dma_start(dst[:, :], w[name]).then_inc(in_w, 16)
            act.wait_ge(in_mod, 48)
            nc.scalar.activation(ce[:, :], ct[:, :], ACT.Exp, scale=-1.0).then_inc(exp_c, 1)
            act.wait_ge(var_ok, 1)
            nc.scalar.activation(m.sd[:, :, :], m.ve[:, :, :], ACT.Sqrt).then_inc(sqrt_ok, 1)
            act.wait_ge(mod_read, 1)
            for c in range(NCH):
                b = c // 2
                act.wait_ge(turn_ok, c + 1)
                nc.scalar.activation(m.cur[:, c, :], turned[c % 2][:, :], ACT.Identity,
                                     bias=m.modc[:, 0, b:b + 1], scale=m.modc[:, 1, b:b + 1]).then_inc(h_ok, 1)
                act.wait_ge(lat_ok, c + 1)
                nc.scalar.activation(lat[:, c % 2, :], plv[0:LAT, :], ACT.Copy).then_inc(lat_sb, 1)
                act.wait_ge(v_ok, c + 1)
                j = TPC * (c % 2)
                for hg in range(NG):
                    v = nc.scalar.activation(
                        m.v[:, b * NG + hg, j:j + TPC, :],
                        plv[:, :].rearrange("p (j g r) -> p j g r", j=TPC, g=NG)[:, :, hg, :], ACT.Copy)
                v.then_inc(v_sb, 1)
                for side in range(2):
                    n = 2 * c + side + 1
                    at = slice(CH * (c % 2), CH * (c % 2) + CH)
                    act.wait_ge(rot, n)
                    nc.scalar.activation(pieces[side][:, b, 0, at], ro[side][:, :], ACT.Copy).then_inc(piece0, 1)
                    act.wait_ge(rest, n)
                    nc.scalar.activation(pieces[side][:, b, 1, at], rr[side][:, :], ACT.Copy).then_inc(piece1, 1)

        @block.gpsimd
        def _(pool):
            for n in range(2 * NCH):
                c, side = n // 2, n % 2
                b = c // 2
                at = slice(CH * (c % 2), CH * (c % 2) + CH)
                pool.wait_ge(piece0, n + 1)
                if n >= 2:
                    pool.wait_ge(piece1, n - 1)
                    pool.wait_ge(piece2, n - 1)
                nc.gpsimd.tensor_tensor(rr[side][:, :], ro[side][:, :], pieces[side][:, b, 0, at],
                                        ALU.subtract).then_inc(rest, 1)
                pool.wait_ge(piece1, n + 1)
                pool.wait_ge(rest, n + 1)
                nc.gpsimd.tensor_tensor(pieces[side][:, b, 2, at], rr[side][:, :], pieces[side][:, b, 1, at],
                                        ALU.subtract).then_inc(piece2, 1)

        @block.vector
        def _(v):
            links = [0]

            def link(ins):
                links[0] += 1
                ins.then_inc(dve, 1)
                v.wait_ge(dve, links[0])

            v.wait_ge(exp_c, 1)
            link(nc.vector.tensor_scalar(ce[:, :], ce[:, :], 1.0, None, ALU.add))
            link(nc.vector.reciprocal(ce[:, :], ce[:, :]))
            nc.vector.tensor_tensor(sc[:, :], ct[:, :], ce[:, :], ALU.mult).then_inc(silu_c, 1)
            nc.vector.tensor_copy(m.identb[:, :], m.ident[:, :])
            for c in range(NCH):
                v.wait_ge(in_x[c], 16)
                for t in range(TPC * c, TPC * c + TPC):
                    s = nc.vector.bn_stats(m.stats[:, t, :], m.x[:, t, :])
            link(s)
            for t in range(NT):
                s = nc.vector.bn_aggr(m.mv[:, t, :], m.stats[:, t, :])
            link(s)

            rstd_steps(nc, v, link, var_ok, sqrt_ok, m)
            for c in range(NCH):
                for t in range(TPC * c, TPC * c + TPC):
                    s = nc.vector.tensor_scalar(xn[:, t, :], m.x[:, t, :], m.mv[:, t, 0:1], m.rstd[:, t, :],
                                                ALU.subtract, ALU.mult)
                s.then_inc(xn_ok, 1)
                if c == 0:
                    v.wait_ge(mods, 1)
                    link(nc.vector.tensor_copy(m.modc[:, :, :],
                                               pmod[:, 0:6 * B].rearrange("p (i b) -> p i b", b=B)))
                    link(nc.vector.tensor_copy(ga[:, :, :], pmod[:, E:E + B * E].rearrange("p (b e) -> p b e", b=B)))
                    for i in (1, 4):
                        s = nc.vector.tensor_scalar(m.modc[:, i, :], m.modc[:, i, :], 1.0, None, ALU.add)
                    s.then_inc(mod_read, 1)
                    v.wait_ge(in_w, 80)
                    for dst, src in ((wqs, wq), (wks, wk)):
                        pd, ps = (a[:, :].rearrange("p (i two) -> p i two", two=2) for a in (dst, src))
                        nc.vector.tensor_scalar(pd[:, :, 0:1], ps[:, :, 1:2], -1.0, None, ALU.mult)
                        s = nc.vector.tensor_copy(pd[:, :, 1:2], ps[:, :, 0:1])
                    s.then_inc(swap_ok, 1)
            v.wait_ge(in_tab, 32)
            for c in range(NCH):
                tab = slice(CH * (c % 2), CH * (c % 2) + CH)
                for side, (ready, pp) in enumerate(((q_ok, pq), (k_ok, pk))):
                    n = 2 * c + side
                    v.wait_ge(ready, c + 1)
                    nc.vector.tensor_tensor(rc[side][:, :], pp[0][:, :], cos[:, tab], ALU.mult)
                    s = nc.vector.tensor_tensor(rs[side][:, :], pp[1][:, :], sin[:, tab], ALU.mult)
                    s.then_inc(rot_read, 1)
                    v.wait_ge(rot_read, n + 1)
                    if n >= 2:
                        v.wait_ge(piece0, n - 1)
                        v.wait_ge(rest, n - 1)
                    nc.vector.tensor_tensor(ro[side][:, :], rc[side][:, :], rs[side][:, :], ALU.add).then_inc(rot, 1)
            for g, t, s in ((ga[:, :, :], gt[:, :, :], gs[:, :, :]), (m.modc[:, 5, :], bt[:, :], bs[:, :])):
                link(nc.vector.tensor_scalar(t, g, -1.0, None, ALU.mult))
                link(nc.vector.tensor_tensor(t, t, g, ALU.max))
                link(nc.vector.tensor_scalar(t, t, 0.25, None, ALU.max))
                link(nc.vector.tensor_scalar(s, g, 0.0, 2.0, ALU.is_ge, ALU.mult))
                link(nc.vector.tensor_scalar(s, s, -1.0, None, ALU.add))
                link(nc.vector.tensor_tensor(t, t, s, ALU.mult))
            for b in range(B):
                nc.vector.tensor_tensor(m.wog[:, b, :], wo[:, :], gt[:, b, :], ALU.mult)
                nc.vector.tensor_scalar(m.gbd[:, b, :], m.ident[:, :], bt[:, b:b + 1], None, ALU.mult)

        @block.tensor
        def _(pe):
            pe.wait_ge(silu_c, 1)
            for i in range(6):
                nc.tensor.matmul(pmod[:, i * B:(i + 1) * B], wmod[:, i * E:(i + 1) * E], sc[:, :], start=True, stop=True)
            for b in range(B):
                mm = nc.tensor.matmul(pmod[:, E + b * E:E + (b + 1) * E], sc[:, b:b + 1].broadcast_to([P, P]),
                                      wmod[:, 2 * E:3 * E], start=True, stop=True)
            mm.then_inc(mods, 1)
            for c in range(NCH):
                pe.wait_ge(xn_ok, c + 1)
                if c >= 2:
                    pe.wait_ge(h_ok, c - 1)
                for i in range(TPC):
                    mm = nc.tensor.transpose(turned[c % 2][:, i * P:(i + 1) * P], xn[:, TPC * c + i, :], m.ident[:, :])
                mm.then_inc(turn_ok, 1)
                pe.wait_ge(h_ok, c + 1)
                pe.wait_ge(swap_ok, 1)
                if c >= 1:
                    pe.wait_ge(v_sb, c)
                    pe.wait_ge(rot_read, 2 * c)
                nc.tensor.matmul(plv[0:LAT, :], wd[:, :], m.cur[:, c, :], start=True, stop=True).then_inc(lat_ok, 1)
                nc.tensor.matmul(pq[0][:, :], wq[:, :], m.cur[:, c, :], start=True, stop=True)
                nc.tensor.matmul(pq[1][:, :], wqs[:, :], m.cur[:, c, :], start=True, stop=True).then_inc(q_ok, 1)
                pe.wait_ge(lat_sb, c + 1)
                nc.tensor.matmul(pk[0][:, :], wk[:, :], lat[:, c % 2, :], start=True, stop=True)
                nc.tensor.matmul(pk[1][:, :], wks[:, :], lat[:, c % 2, :], start=True, stop=True).then_inc(k_ok, 1)
                for i in range(TPC):
                    mm = nc.tensor.matmul(plv[:, i * P:(i + 1) * P], lat[:, c % 2, i * P:(i + 1) * P], wv[:, :],
                                          start=True, stop=True)
                mm.then_inc(v_ok, 1)


def attention(nc, m, l):
    probs = [l.sb(f"probs{s}", [P, HG, CH]) for s in range(SLOTS)]
    vs = [l.sb(f"vs{s}", [P, JB, HG, 32]) for s in range(SLOTS)]
    mcol = l.sb("mcol", [P, HG, 12])
    mres = l.sb("mres", [P, HG, JB])
    mpc = l.sb("mpc", [P, 3, HG, JB], BF16)
    mrow = l.sb("mrow", [3 * HG * JB, P], BF16)
    w1_raw = l.sb("w1_raw", [P, NE, FF])
    w2_raw = l.sb("w2_raw", [P, NE * FF // P, E])
    st = l.ps("st", [P, HG, CH])
    ov = l.ps("ov", [P, 2, CH])
    mx = l.ps("mx", [P, 2, CH])

    qk_in = [l.sem(f"qk_in{s}") for s in range(SLOTS)]
    mrow_in = [l.sem(f"mrow_in{s}") for s in range(SLOTS)]
    st_done, exp_done, pv_done, ov_read = (l.sem(n) for n in ("st_done", "exp_done", "pv_done", "ov_read"))
    bin_full, bin_read, mchain = (l.sem(n) for n in ("bin_full", "bin_read", "mchain"))
    vs_init, vs_ok, w_in, w_hi, w_lo, small_in = (
        l.sem(n) for n in ("vs_init", "vs_ok", "w_in", "w_hi", "w_lo", "small_in"))
    ST_CREDIT, EXP_CREDIT, PV_CREDIT, OV_CREDIT = 1, 2, SLOTS, 2
    CHAIN = 6

    def gnum(i, a):
        return SLOTS * i + a

    def exists(i, a):
        return not isinstance(i, int) or SLOTS * i + a < GROUPS

    def uses(i, a):
        return i + (a // SLOTS + 1)

    def all_groups(eng, body):
        whole = (GROUPS - 2) // SLOTS
        with eng.Fori(0, whole) as i:
            for a in range(SLOTS):
                body(i, a)
        for g in range(whole * SLOTS, GROUPS):
            body(whole, g - whole * SLOTS)

    def following(i, a, u):
        return (i, a, u + 1) if u + 1 < NU else (i, a + 1, 0)

    def part_at(i, a, u):
        n = u + LEAD
        return (i, a + 1, n) if n < NU else (i, a + 2, n - NU)

    with nc.Block() as block:

        @block.sync
        def _(sp):
            def load(i, a):
                s, g = a % SLOTS, gnum(i, a)
                for term in range(TERMS):
                    rows = slice(term * D, term * D + D)
                    sp.dma_start(m.ks[s][rows, :, :],
                                 m.kp[g, K_PIECE[term]].rearrange("(h d) t -> d h t", d=D)).then_inc(qk_in[s], 16)
                    sp.dma_start(m.qs[s][rows, :, :],
                                 m.qp[g, Q_PIECE[term]].rearrange("(h d) t -> d h t", d=D)).then_inc(qk_in[s], 16)

            def max_rows(i, a):
                s = a % SLOTS
                sp.wait_ge(bin_read, NB * gnum(i, a) + NB)
                sp.dma_start(m.qs[s][ROW_MAX:ROW_MAX + 3, :, :], mrow[:, :]).then_inc(mrow_in[s], 16)

            def body(i, a):
                if exists(i, a + 2):
                    sp.wait_ge(st_done, 2 * NU * gnum(i, a) + ST_CREDIT)
                    load(i, a + 2)
                if exists(i, a + 1):
                    max_rows(i, a + 1)

            load(0, 0)
            load(0, 1)
            max_rows(0, 0)
            sp.dma_start(w1_raw[:, :, :], m.w["W1"].rearrange("e h f -> h e f")).then_inc(w_in, 16)
            sp.dma_start(w2_raw[:, :, :], m.w["W2"].rearrange("e (c f) h -> f (e c) h", f=P)).then_inc(w_in, 16)
            sp.dma_start(m.wg[:, :, :], m.w["Wg"]).then_inc(small_in, 16)
            sp.dma_start(m.bg[:, :, :, :], m.w["bg"]).then_inc(small_in, 16)
            sp.dma_start(m.b1[:, :, :], m.w["b1"]).then_inc(small_in, 16)
            sp.dma_start(m.b2[:, :], m.w["b2"]).then_inc(small_in, 16)
            sp.dma_start(m.tri[:, :, :, :], m.w["tri"]).then_inc(small_in, 16)
            all_groups(sp, body)
            sp.wait_ge(small_in, 80)

        @block.gpsimd
        def _(pool):
            def stage(i, a):
                s = a % SLOTS
                nc.gpsimd.tensor_copy(vs[s][:, :, :, 0:D],
                                      m.v[:, gnum(i, a), :, :].rearrange("p j (h d) -> p j h d", d=D)).then_inc(vs_ok, 1)

            for s in range(SLOTS):
                nc.gpsimd.memset(vs[s][:, :, :, :], 0.0).then_inc(vs_init, 1)
            pool.wait_ge(vs_init, SLOTS)
            for s in range(SLOTS):
                nc.gpsimd.memset(vs[s][:, :, :, D:D + 1], 1.0).then_inc(vs_init, 1)
            pool.wait_ge(vs_init, 2 * SLOTS)
            stage(0, 0)
            stage(0, 1)
            pool.wait_ge(w_in, 32)
            for e in range(NE):
                c = slice(e * FF // P, (e + 1) * FF // P)
                nc.gpsimd.tensor_copy(m.w1_hi[:, e, :], w1_raw[:, e, :])
                nc.gpsimd.tensor_copy(m.w2_hi[:, c, :], w2_raw[:, c, :]).then_inc(w_hi, 1)
                pool.wait_ge(w_hi, e + 1)
                nc.gpsimd.tensor_tensor(m.w1_lo[:, e, :], w1_raw[:, e, :], m.w1_hi[:, e, :], ALU.subtract)
                nc.gpsimd.tensor_tensor(m.w2_lo[:, c, :], w2_raw[:, c, :], m.w2_hi[:, c, :],
                                        ALU.subtract).then_inc(w_lo, 1)

            def body(i, a):
                if exists(i, a + 2):
                    pool.wait_ge(vs_init, 2 * SLOTS)
                    pool.wait_ge(pv_done, NU * gnum(i, a) + PV_CREDIT)
                    stage(i, a + 2)

            all_groups(pool, body)

        @block.scalar
        def _(act):
            def exps(i, a, u):
                n = NU * gnum(i, a) + u
                for half in range(2):
                    h = slice(2 * half, 2 * half + 2)
                    act.wait_ge(st_done, 2 * n + half + 1 + ST_CREDIT)
                    if half == 0:
                        act.wait_ge(pv_done, n + 1 - SLOTS + PV_CREDIT)
                    nc.scalar.activation(probs[u % SLOTS][:, h, :], st[:, h, :], ACT.Exp,
                                         scale=SCALE).then_inc(exp_done, 1)

            def keep_output(i, a, c):
                g = gnum(i, a)
                act.wait_ge(pv_done, NU * g + LAST_UNIT[c] + 1 + PV_CREDIT)
                nc.scalar.activation(m.ovs[:, g, c, :], ov[:, c, :], ACT.Copy).then_inc(ov_read, 1)

            def body(i, a):
                for u in range(NU):
                    if exists(*following(i, a, u)[:2]):
                        exps(*following(i, a, u))
                    if u == LAST_UNIT[0] + 1:
                        keep_output(i, a, 0)
                keep_output(i, a, 1)

            exps(0, 0, 0)
            all_groups(act, body)

        @block.vector
        def _(v):
            def read_bin(i, a, k):
                h, b = GROUP_BINS[k]
                blocks, keys, slot, step = BINS[b]
                n = NB * gnum(i, a) + k
                v.wait_ge(bin_full, n + 1)
                nc.vector.tensor_reduce(mcol[:, h, slot:slot + step * (len(blocks) - 1) + 1:step],
                                        mx[:, k % 2, 0:len(blocks) * keys].rearrange("p (b k) -> p b k", k=keys),
                                        AX.X, ALU.max, negate=True).then_inc(bin_read, 1)

            def maxima(i, a):
                g = gnum(i, a)
                at = [CHAIN * g]

                def link(ins):
                    at[0] = at[0] + 1
                    ins.then_inc(mchain, 1)
                    v.wait_ge(mchain, at[0])

                v.wait_ge(bin_read, NB * g + NB - 1)
                nm = mcol[:, :, 0:JB]
                link(nc.vector.tensor_tensor(mcol[:, :, 4:8], mcol[:, :, 4:8], mcol[:, :, 8:12], ALU.min))
                link(nc.vector.tensor_copy(mpc[:, 0, :, :], nm))
                link(nc.vector.tensor_tensor(mres[:, :, :], nm, mpc[:, 0, :, :], ALU.subtract))
                link(nc.vector.tensor_copy(mpc[:, 1, :, :], mres[:, :, :]))
                link(nc.vector.tensor_tensor(mres[:, :, :], mres[:, :, :], mpc[:, 1, :, :], ALU.subtract))
                link(nc.vector.tensor_copy(mpc[:, 2, :, :], mres[:, :, :]))
                v.wait_ge(bin_full, NB * g + NB)
                if not isinstance(i, int) or SLOTS * i + a > 0:
                    s = (a - 1) % SLOTS
                    v.wait_ge(mrow_in[s], 16 * uses(i, a - 1))
                nc.vector.tensor_copy(mrow[:, :], mx[0:3 * HG * JB, (NB - 1) % 2, 0:P // 2].bitcast(BF16))\
                    .then_inc(bin_read, 1)

            def part(i, a, p):
                for k in range(BEFORE[p], BEFORE[p] + len(PARTS[p])):
                    read_bin(i, a, k)
                if p == NU - 1:
                    maxima(i, a)

            def body(i, a):
                for u in range(NU):
                    if exists(*part_at(i, a, u)[:2]):
                        part(*part_at(i, a, u))

            for p in range(NU):
                part(0, 0, p)
            for p in range(LEAD):
                part(0, 1, p)
            all_groups(v, body)

        @block.tensor
        def _(pe):
            def scores(i, a, u, half):
                s, n = a % SLOTS, NU * gnum(i, a) + u
                if u == 0 and half == 0:
                    pe.wait_ge(qk_in[s], 16 * 2 * TERMS * uses(i, a))
                    pe.wait_ge(mrow_in[s], 16 * uses(i, a))
                pe.wait_ge(exp_done, 2 * n - 1 + half + EXP_CREDIT)
                for h in (2 * half, 2 * half + 1):
                    for c, j, off, q0, nq in UNITS[u]:
                        mm = nc.tensor.matmul(st[:, h, off:off + nq], m.ks[s][:, h, j * P:(j + 1) * P],
                                              m.qs[s][:, h, c * CH + q0:c * CH + q0 + nq], start=True, stop=True)
                mm.then_inc(st_done, 1)

            def weigh(i, a, u):
                s, g = a % SLOTS, gnum(i, a)
                pe.wait_ge(exp_done, 2 * (NU * g + u + 1) + EXP_CREDIT)
                if u == FIRST_UNIT[0]:
                    pe.wait_ge(vs_ok, g + 1)
                for c in range(2):
                    if u == FIRST_UNIT[c]:
                        pe.wait_ge(ov_read, 2 * g - 1 + c + OV_CREDIT)
                for c, j, off, q0, nq in UNITS[u]:
                    for h in range(HG):
                        mm = nc.tensor.matmul(ov[32 * h:32 * h + 32, c, q0:q0 + nq], vs[s][:, j, h, :],
                                              probs[u % SLOTS][:, h, off:off + nq],
                                              start=(u == FIRST_UNIT[c]), stop=(u == LAST_UNIT[c]),
                                              skip_group_check=True)
                mm.then_inc(pv_done, 1)

            def fill_bin(i, a, k):
                s, n = a % SLOTS, NB * gnum(i, a) + k
                h, b = GROUP_BINS[k]
                if k == 0:
                    pe.wait_ge(qk_in[s], 16 * 2 * TERMS * uses(i, a))
                if not isinstance(n, int) or n >= 2:
                    pe.wait_ge(bin_read, n if k == 0 else n - 1)
                blocks, keys, _, _ = BINS[b]
                for x, (t, k0) in enumerate(blocks):
                    mm = nc.tensor.matmul(mx[:, k % 2, x * keys:(x + 1) * keys],
                                          m.qs[s][0:ROW_MAX, h, t * P:(t + 1) * P],
                                          m.ks[s][0:ROW_MAX, h, k0:k0 + keys], start=True, stop=True)
                mm.then_inc(bin_full, 1)

            def turn_maxima(i, a):
                g = gnum(i, a)
                pe.wait_ge(mchain, CHAIN * g + CHAIN)
                pe.wait_ge(bin_read, NB * g + NB - 2)
                nc.tensor.transpose(mx[0:3 * HG * JB, (NB - 1) % 2, 0:P // 2].bitcast(BF16),
                                    mpc[:, :, :, :].rearrange("p c h t -> p (c h t)"),
                                    m.identb[:, :]).then_inc(bin_full, 1)

            def part(i, a, p, half):
                ks = range(BEFORE[p], BEFORE[p] + len(PARTS[p]))
                cut = len(PARTS[p]) // 2
                for k in (ks[:cut] if half == 0 else ks[cut:]):
                    fill_bin(i, a, k)

            def body(i, a):
                for u in range(NU):
                    nxt, side = following(i, a, u), part_at(i, a, u)
                    if side[2] == 0 and exists(i, a + 1):
                        turn_maxima(i, a + 1)
                    for half in range(2):
                        if exists(*nxt[:2]):
                            scores(*nxt, half)
                        if exists(*side[:2]):
                            part(*side, half)
                    weigh(i, a, u)

            nc.tensor.sem_inc(st_done, ST_CREDIT)
            nc.tensor.sem_inc(exp_done, EXP_CREDIT)
            nc.tensor.sem_inc(pv_done, PV_CREDIT)
            nc.tensor.sem_inc(ov_read, OV_CREDIT)
            for p in range(NU):
                part(0, 0, p, 0)
                part(0, 0, p, 1)
            turn_maxima(0, 0)
            for p in range(LEAD):
                part(0, 1, p, 0)
                part(0, 1, p, 1)
            scores(0, 0, 0, 0)
            scores(0, 0, 0, 1)
            all_groups(pe, body)


def project(nc, m, l):
    rec = l.sb("rec", [P, 2, NH, 1])
    att = l.sb("att", [P, 2, NH, D])
    att_t = l.sb("att_t", [P, 2, P])
    xn = l.sb("xn2", [P, NT, E])
    heads = [l.ps(f"heads{i}", [P, CH]) for i in range(2)]
    turn = [l.ps(f"turn{i}", [P, CH]) for i in range(2)]
    added = [l.ps(f"added{i}", [P, CH]) for i in range(2)]
    h_t = [l.ps(f"h_t{i}", [P, CH]) for i in range(2)]
    heads_ok, rec_ok, att_ok, turn_ok, att_sb, add_ok, x_ok = (
        l.sem(n) for n in ("heads_ok", "rec_ok", "att_ok", "turn2_ok", "att_sb", "add_ok", "x_ok"))
    dve, var_ok, sqrt_ok, xn_ok, ht_ok, h_ok = (
        l.sem(n) for n in ("dve_proj", "var2_ok", "sqrt2_ok", "xn2_ok", "ht_ok", "h2_ok"))

    with nc.Block() as block:

        @block.tensor
        def _(pe):
            def to_tokens(t):
                if t >= 2:
                    pe.wait_ge(att_ok, t - 1)
                b, c, i = t // JB, t % JB // TPC, t % TPC
                for hg in range(NG):
                    mm = nc.tensor.transpose(heads[t % 2][:, hg * P:(hg + 1) * P],
                                             m.ovs[:, b * NG + hg, c, i * P:(i + 1) * P], m.ident[:, :])
                mm.then_inc(heads_ok, 1)

            def back(t):
                pe.wait_ge(att_ok, t + 1)
                if t >= 2:
                    pe.wait_ge(att_sb, t - 1)
                nc.tensor.transpose(turn[t % 2][:, 0:P], att[:, t % 2, :, :].rearrange("p h d -> p (h d)"),
                                    m.ident[:, :]).then_inc(turn_ok, 1)

            def wo(t):
                pe.wait_ge(att_sb, t + 1)
                if t >= 2:
                    pe.wait_ge(x_ok, t - 1)
                nc.tensor.matmul(added[t % 2][:, 0:E], att_t[:, t % 2, :], m.wog[:, t // JB, :],
                                 start=True, stop=True).then_inc(add_ok, 1)

            for t in range(NT + 2):
                if t < NT:
                    to_tokens(t)
                if 1 <= t <= NT:
                    back(t - 1)
                if t >= 2:
                    wo(t - 2)
            for c in range(NCH):
                pe.wait_ge(xn_ok, c + 1)
                if c >= 2:
                    pe.wait_ge(h_ok, c - 1)
                for i in range(TPC):
                    mm = nc.tensor.transpose(h_t[c % 2][:, i * P:(i + 1) * P], xn[:, TPC * c + i, :], m.ident[:, :])
                mm.then_inc(ht_ok, 1)

        @block.scalar
        def _(act):
            for t in range(NT):
                act.wait_ge(turn_ok, t + 1)
                if t >= 2:
                    act.wait_ge(add_ok, t - 1)
                nc.scalar.activation(att_t[:, t % 2, :], turn[t % 2][:, 0:P], ACT.Copy).then_inc(att_sb, 1)
            act.wait_ge(var_ok, 1)
            nc.scalar.activation(m.sd[:, :, :], m.ve[:, :, :], ACT.Sqrt).then_inc(sqrt_ok, 1)
            for c in range(NCH):
                b = c // 2
                act.wait_ge(ht_ok, c + 1)
                nc.scalar.activation(m.cur[:, c, :], h_t[c % 2][:, :], ACT.Identity,
                                     bias=m.modc[:, 3, b:b + 1], scale=m.modc[:, 4, b:b + 1]).then_inc(h_ok, 1)

        @block.vector
        def _(v):
            links = [0]

            def link(ins):
                links[0] += 1
                ins.then_inc(dve, 1)
                v.wait_ge(dve, links[0])

            def divide(t):
                v.wait_ge(heads_ok, t + 1)
                if t >= 2:
                    v.wait_ge(turn_ok, t - 1)
                o = heads[t % 2][:, :].rearrange("p (h r) -> p h r", r=32)
                nc.vector.reciprocal(rec[:, t % 2, :, :], o[:, :, D:D + 1]).then_inc(rec_ok, 1)
                v.wait_ge(rec_ok, t + 1)
                nc.vector.tensor_tensor(att[:, t % 2, :, :], o[:, :, 0:D],
                                        rec[:, t % 2, :, :].broadcast_to([P, NH, D]), ALU.mult).then_inc(att_ok, 1)

            def residual(t):
                v.wait_ge(add_ok, t + 1)
                nc.vector.tensor_tensor(m.x[:, t, :], m.x[:, t, :], added[t % 2][:, 0:E], ALU.add).then_inc(x_ok, 1)
                v.wait_ge(x_ok, t + 1)
                return nc.vector.bn_stats(m.stats[:, t, :], m.x[:, t, :])

            for t in range(NT + 2):
                if t < NT:
                    divide(t)
                if t >= 2:
                    last = residual(t - 2)
            link(last)
            for t in range(NT):
                last = nc.vector.bn_aggr(m.mv[:, t, :], m.stats[:, t, :])
            link(last)
            rstd_steps(nc, v, link, var_ok, sqrt_ok, m)
            for c in range(NCH):
                for t in range(TPC * c, TPC * c + TPC):
                    last = nc.vector.tensor_scalar(xn[:, t, :], m.x[:, t, :], m.mv[:, t, 0:1], m.rstd[:, t, :],
                                                   ALU.subtract, ALU.mult)
                last.then_inc(xn_ok, 1)


def ffn(nc, m, l):
    K = NE * FF // P
    NS = NCH * K
    AHEAD, RING = 2, 4
    cur_hi = l.sb("cur_hi", [P, NCH, CH], F32R)
    cur_lo = l.sb("cur_lo", [P, NCH, CH], F32R)
    gel = [l.sb(f"gel{i}", [P, CH]) for i in range(RING)]
    gel_hi = [l.sb(f"gel_hi{i}", [P, CH], F32R) for i in range(RING)]
    gel_lo = [l.sb(f"gel_lo{i}", [P, CH], F32R) for i in range(RING)]
    cwb = l.sb("cwb", [P, NE, CH])
    part = l.sb("part", [P, 2, CH])
    log = l.sb("log", [P, TPC, NE])
    ge, gt = l.sb("at_least", [P, TPC, NE, NE]), l.sb("above", [P, TPC, NE, NE])
    rank, half, hdiff, dl = (l.sb(n, [P, TPC, NE]) for n in ("rank", "half", "hdiff", "dl"))
    gap, th = l.sb("gap", [P, TPC, 1]), l.sb("th", [P, TPC, 1])
    cw = l.sb("cw", [P, TPC, NE])
    hid = [l.ps(f"hid{i}", [P, CH]) for i in range(RING)]
    y = [l.ps(f"y{i}", [P, CH]) for i in range(2)]
    plog = l.ps("plog", [P, CH])
    pcw = l.ps("pcw", [P, CH])

    cur_ok, hi_ok, hid_ok, gel_ok, lo_ok, y_ok = (
        l.sem(n) for n in ("cur_ok", "hi_ok", "hid_ok", "gel_ok", "lo_ok", "y_ok"))
    log_ok, gap_ok, th_ok, cw_ok, pcw_ok, cwb_ok, part_ok, add_ok, chain = (
        l.sem(n) for n in ("log_ok", "gap_ok", "th_ok", "cw_ok", "pcw_ok", "cwb_ok", "part_ok", "addf_ok", "chain"))
    last_ok, out_ok, stored = (l.sem(n) for n in ("last_ok", "out_ok", "stored"))
    GEL_CREDIT, Y_CREDIT, PART_CREDIT, ADD_CREDIT, CWB_CREDIT = RING, RING, 2, 2, 1
    LINKS = 9

    def split_step(s):
        return s // K, s % K // (FF // P), s % (FF // P)

    def base(c):
        return max(K * c - 4, 0)

    LOGITS = {base(c): c for c in range(NCH)}
    RANKS = {base(c) + 1: c for c in range(NCH)}
    TANH = {base(c) + 3: c for c in range(NCH)}
    WEIGHTS = {base(c) + 4: c for c in range(NCH)}
    SPREAD = {base(c) + 6 + e: (c, e) for c in range(NCH) for e in range(NE)}
    KEEP = {base(c) + 8 + e: (c, e) for c in range(NCH) for e in range(NE)}
    COMBINE = {min(max(base(c) + 9 + e, K * c + 4 * e + 4), NS - 1): (c, e) for c in range(NCH) for e in range(NE)}

    with nc.Block() as block:

        @block.tensor
        def _(pe):
            def up(r, s):
                if s >= NS:
                    r, s = r + 1, s - NS
                c, e, q = split_step(s)
                if s % K == 0:
                    pe.wait_ge(cur_ok, NCH * r + c + 1)
                pe.wait_ge(gel_ok, NS * r + s - RING + 1 + GEL_CREDIT)
                f = slice(q * P, (q + 1) * P)
                h = hid[s % RING][:, :]
                nc.tensor.matmul(h, m.w1_hi[:, e, f], cur_hi[:, c, :], start=True, stop=False)
                nc.tensor.matmul(h, m.w1_hi[:, e, f], cur_lo[:, c, :], start=False, stop=False)
                nc.tensor.matmul(h, m.w1_lo[:, e, f], cur_hi[:, c, :], start=False, stop=True).then_inc(hid_ok, 1)

            def down(r, s):
                c, e, q = split_step(s)
                n = NE * (NCH * r + c) + e
                if q == 0:
                    pe.wait_ge(part_ok, n - 1 + PART_CREDIT)
                pe.wait_ge(lo_ok, NS * r + s + 1)
                o, x, first, last = y[e % 2][:, :], e * (FF // P) + q, q == 0, q == FF // P - 1
                nc.tensor.matmul(o, m.w2_hi[:, x, :], gel_hi[s % RING][:, :], start=first, stop=False)
                nc.tensor.matmul(o, m.w2_lo[:, x, :], gel_hi[s % RING][:, :], start=False, stop=False)
                nc.tensor.matmul(o, m.w2_hi[:, x, :], gel_lo[s % RING][:, :], start=False, stop=last).then_inc(y_ok, 1)

            def logits(r, c):
                pe.wait_ge(cur_ok, NCH * r + c + 1)
                for i in range(TPC):
                    mm = nc.tensor.matmul(plog[:, i * NE:(i + 1) * NE], m.cur[:, c, i * P:(i + 1) * P],
                                          m.wg[:, r, :], start=True, stop=True)
                mm.then_inc(log_ok, 1)

            def spread(r, c, e):
                n = NE * (NCH * r + c) + e
                pe.wait_ge(cw_ok, NCH * r + c + 1)
                pe.wait_ge(cwb_ok, n + CWB_CREDIT)
                for i in range(TPC):
                    mm = nc.tensor.transpose(pcw[:, i * P:(i + 1) * P], cw[:, i, e:e + 1].broadcast_to([P, P]),
                                             m.ident[:, :])
                mm.then_inc(pcw_ok, 1)

            nc.tensor.sem_inc(gel_ok, GEL_CREDIT)
            nc.tensor.sem_inc(y_ok, Y_CREDIT)
            nc.tensor.sem_inc(part_ok, PART_CREDIT)
            nc.tensor.sem_inc(add_ok, ADD_CREDIT)
            nc.tensor.sem_inc(cwb_ok, CWB_CREDIT)
            for s in range(AHEAD):
                up(0, s)
            with pe.Fori(0, R) as r:
                for s in range(NS):
                    up(r, s + AHEAD)
                    if s in LOGITS:
                        logits(r, LOGITS[s])
                    if s in SPREAD:
                        spread(r, *SPREAD[s])
                    down(r, s)
            for c in range(NCH):
                pe.wait_ge(cur_ok, NCH * R + c + 1)
                if c == 0:
                    pe.wait_ge(gel_ok, NS * R + GEL_CREDIT)
                for i in range(TPC):
                    mm = nc.tensor.matmul(hid[(c + 2) % RING][:, i * P:(i + 1) * P], m.cur[:, c, i * P:(i + 1) * P],
                                          m.gbd[:, c // 2, :], start=True, stop=True)
                mm.then_inc(last_ok, 1)

        @block.scalar
        def _(act):
            def gelu(r, s):
                c, e, q = split_step(s)
                act.wait_ge(hid_ok, NS * r + s + 1)
                act.wait_ge(y_ok, NS * r + s - RING + 1 + Y_CREDIT)
                bias = m.b1[:, e, q:q + 1]
                nc.scalar.activation(gel[s % RING][:, :], hid[s % RING][:, :], ACT.Gelu_apprx_tanh, bias=bias)
                nc.scalar.activation(gel_hi[s % RING][:, :], hid[s % RING][:, :], ACT.Gelu_apprx_tanh,
                                     bias=bias).then_inc(gel_ok, 1)

            def keep(r, c, e):
                n = NE * (NCH * r + c) + e
                act.wait_ge(pcw_ok, n + 1)
                nc.scalar.activation(cwb[:, e, :], pcw[:, :], ACT.Copy).then_inc(cwb_ok, 1)

            with act.Fori(0, R) as r:
                for s in range(NS):
                    gelu(r, s)
                    if s in TANH:
                        act.wait_ge(gap_ok, NCH * r + TANH[s] + 1)
                        nc.scalar.activation(th[:, :, :], gap[:, :, :], ACT.Tanh).then_inc(th_ok, 1)
                    if s in KEEP:
                        keep(r, *KEEP[s])

        @block.vector
        def _(v):
            def low(r, s):
                v.wait_ge(gel_ok, NS * r + s + 1 + GEL_CREDIT)
                nc.vector.tensor_tensor(gel_lo[s % RING][:, :], gel[s % RING][:, :], gel_hi[s % RING][:, :],
                                        ALU.subtract).then_inc(lo_ok, 1)

            def linker(r, c, at):
                at = [at]

                def link(ins):
                    at[0] += 1
                    ins.then_inc(chain, 1)
                    v.wait_ge(chain, LINKS * (NCH * r + c) + at[0])
                return link

            def ranks(r, c):
                link = linker(r, c, 0)
                v.wait_ge(log_ok, NCH * r + c + 1)
                link(nc.vector.tensor_tensor(log[:, :, :], plog[:, 0:TPC * NE].rearrange("p (t e) -> p t e", e=NE),
                                             m.bg[:, r, :, :].broadcast_to([P, TPC, NE]), ALU.add))
                other = log[:, :, :].rearrange("p t (e j) -> p t e j", e=1).broadcast_to([P, TPC, NE, NE])
                own = log[:, :, :].rearrange("p t (e j) -> p t e j", j=1).broadcast_to([P, TPC, NE, NE])
                nc.vector.tensor_tensor(ge[:, :, :, :], other, own, ALU.is_ge)
                link(nc.vector.tensor_tensor(gt[:, :, :, :], other, own, ALU.is_gt))
                tri = [m.tri[:, i:i + 1, :, :].broadcast_to([P, TPC, NE, NE]) for i in range(2)]
                nc.vector.tensor_tensor(ge[:, :, :, :], ge[:, :, :, :], tri[0], ALU.mult)
                link(nc.vector.tensor_tensor(gt[:, :, :, :], gt[:, :, :, :], tri[1], ALU.mult))
                link(nc.vector.tensor_tensor(ge[:, :, :, :], ge[:, :, :, :], gt[:, :, :, :], ALU.add))
                link(nc.vector.tensor_reduce(rank[:, :, :], ge[:, :, :, :], AX.X, ALU.add))
                nc.vector.tensor_scalar(half[:, :, :], rank[:, :, :], 1.5, 0.5, ALU.is_lt, ALU.mult)
                link(nc.vector.tensor_scalar(hdiff[:, :, :], rank[:, :, :], 0.5, None, ALU.is_lt))
                link(nc.vector.tensor_tensor(hdiff[:, :, :], hdiff[:, :, :], half[:, :, :], ALU.subtract))
                link(nc.vector.tensor_tensor(dl[:, :, :], hdiff[:, :, :], log[:, :, :], ALU.mult))
                nc.vector.tensor_reduce(gap[:, :, :], dl[:, :, :], AX.X, ALU.add).then_inc(gap_ok, 1)

            def weights(r, c):
                link = linker(r, c, LINKS - 1)
                v.wait_ge(th_ok, NCH * r + c + 1)
                link(nc.vector.tensor_tensor(cw[:, :, :], hdiff[:, :, :], th[:, :, :].broadcast_to([P, TPC, NE]),
                                             ALU.mult))
                nc.vector.tensor_tensor(cw[:, :, :], cw[:, :, :], half[:, :, :], ALU.add).then_inc(cw_ok, 1)

            def combine(r, c, e):
                n = NE * (NCH * r + c) + e
                v.wait_ge(y_ok, NS * r + K * c + (e + 1) * (FF // P) + Y_CREDIT)
                v.wait_ge(cwb_ok, n + 1 + CWB_CREDIT)
                v.wait_ge(add_ok, n - 1 + ADD_CREDIT)
                nc.vector.scalar_tensor_tensor(out=part[:, e % 2, :], in0=y[e % 2][:, :], scalar=m.b2[:, e:e + 1],
                                               in1=cwb[:, e, :], op0=ALU.add, op1=ALU.mult).then_inc(part_ok, 1)

            with v.Fori(0, R) as r:
                for s in range(NS):
                    low(r, s)
                    if s in RANKS:
                        ranks(r, RANKS[s])
                    if s in WEIGHTS:
                        weights(r, WEIGHTS[s])
                    if s in COMBINE:
                        combine(r, *COMBINE[s])
            for c in range(NCH):
                v.wait_ge(last_ok, c + 1)
                xs = m.x[:, TPC * c:TPC * (c + 1), :]
                nc.vector.tensor_tensor(xs, xs, hid[(c + 2) % RING][:, :].rearrange("p (t e) -> p t e", e=E),
                                        ALU.add).then_inc(out_ok, 1)

        @block.gpsimd
        def _(pool):
            def parts(c, n):
                nc.gpsimd.tensor_copy(cur_hi[:, c, :], m.cur[:, c, :]).then_inc(hi_ok, 1)
                pool.wait_ge(hi_ok, n + 1)
                nc.gpsimd.tensor_tensor(cur_lo[:, c, :], m.cur[:, c, :], cur_hi[:, c, :],
                                        ALU.subtract).then_inc(cur_ok, 1)

            for c in range(NCH):
                parts(c, c)
            with pool.Fori(0, R) as r:
                for c in range(NCH):
                    for e in range(NE):
                        n = NE * (NCH * r + c) + e
                        pool.wait_ge(part_ok, n + 1 + PART_CREDIT)
                        pool.wait_ge(add_ok, n + ADD_CREDIT)
                        nc.gpsimd.tensor_tensor(m.cur[:, c, :], m.cur[:, c, :], part[:, e % 2, :],
                                                ALU.add).then_inc(add_ok, 1)
                    pool.wait_ge(hi_ok, NCH)
                    pool.wait_ge(add_ok, n + 1 + ADD_CREDIT)
                    parts(c, NCH * (r + 1) + c)

        @block.sync
        def _(sp):
            for c in range(NCH):
                sp.wait_ge(out_ok, c + 1)
                sp.dma_start(m.out.rearrange("b (t p) e -> p (b t) e", p=P)[:, TPC * c:TPC * (c + 1), :],
                             m.x[:, TPC * c:TPC * (c + 1), :]).then_inc(stored, 16)
            sp.wait_ge(stored, 16 * NCH)


def constants():
    def bf16_bits(a):
        return np.ascontiguousarray(a, np.float32).view(np.uint32) >> 16

    inv = 1.0 / 10000.0 ** (np.arange(0, D, 2, dtype=np.float32) / D)
    ang = np.outer(np.arange(T, dtype=np.float32), inv)
    pair = np.arange(P) % D // 2
    page = np.arange(T) // PAGE
    k_rows = np.zeros((P - ROW_ZERO, T), np.float32)
    k_rows[ROW_PAGE - ROW_ZERO:ROW_PAGE - ROW_ZERO + NPAGE] = page[None, :] == np.arange(NPAGE)[:, None]
    k_rows[ROW_MAX - ROW_ZERO:] = 1.0
    q_rows = np.zeros((ROW_MAX - ROW_ZERO, T), np.float32)
    q_rows[ROW_PAGE - ROW_ZERO:ROW_PAGE - ROW_ZERO + NPAGE] = np.where(page[None, :] < np.arange(NPAGE)[:, None], MASKED, 0.0)
    j, e = np.arange(NE)[None, :], np.arange(NE)[:, None]
    return {
        "cos": np.ascontiguousarray(np.cos(ang).T[pair]),
        "sin": np.ascontiguousarray(np.sin(ang).T[pair]),
        "ident": np.eye(P, dtype=np.float32),
        "k_rows": bf16_bits(k_rows).astype(np.uint16),
        "q_rows": bf16_bits(q_rows).astype(np.uint16),
        "tri": np.broadcast_to(np.stack([j < e, j > e]).astype(np.float32), (P, 2, NE, NE)).copy(),
    }


_INS = {
    "x": "L0_attn_x", "wq": "L0_attn_wq", "w_down": "L0_attn_w_down", "wk_up": "L0_attn_wk_up",
    "wv_up": "L0_attn_wv_up", "wo": "L0_attn_wo", "Wg": "L0_ffn_Wg", "bg": "L0_ffn_bg", "W1": "L0_ffn_W1",
    "b1": "L0_ffn_b1", "W2": "L0_ffn_W2", "b2": "L0_ffn_b2", "c": "L0_c", "wmod": "L0_wmod",
}


def kernel(**inputs):
    import concourse.bacc as bacc
    from concourse.bass_utils import run_bass_kernel_spmd

    nc = bacc.Bacc("TRN2", target_bir_lowering=False, num_devices=1)
    arrays, dram = {}, {}
    given = {name: np.ascontiguousarray(inputs[full]) for name, full in _INS.items()}
    given["c"] = np.ascontiguousarray(given["c"].T)
    given["Wg"] = np.ascontiguousarray(given["Wg"].transpose(1, 0, 2))
    given["bg"] = np.ascontiguousarray(np.broadcast_to(given["bg"][None, :, None, :], (P, R, 1, NE)))
    given["b1"] = np.ascontiguousarray(given["b1"].reshape(NE, FF // P, P).transpose(2, 0, 1))
    given["b2"] = np.ascontiguousarray(given["b2"].T)
    for name, a in {**given, **constants()}.items():
        arrays[f"in_{name}"] = a
        dram[name] = nc.dram_tensor(f"in_{name}", a.shape, mybir.dt.from_np(a.dtype), kind="ExternalInput").ap()
    out = nc.dram_tensor("out", (B, T, E), F32, kind="ExternalOutput").ap()
    adaln_block(nc, dram, out)
    return run_bass_kernel_spmd(nc, [arrays], core_ids=[0]).results[0]["out"]
```

```python
import concourse.bass as bass
import numpy as np
from concourse import mybir
from contextlib import ExitStack

F32 = mybir.dt.float32
F32R = mybir.dt.float32r
BF16 = mybir.dt.bfloat16
ALU = mybir.AluOpType
ACT = mybir.ActivationFunctionType
AX = mybir.AxisListType

P = 128
B, T, E = 2, 1024, 128
NH, D = 16, 8
LAT = 64
NE, R, FF = 4, 4, 512
PAGE = 32
TOK = B * T
NT = TOK // P
CH = 512
NCH = TOK // CH
TPC = CH // P
JB = T // P
HG = 4
NG = NH // HG
GROUPS = B * NG
SLOTS = 3
SCALE = float(D) ** -0.5
EPS = 1e-5

Q_PIECE = [0, 0, 0, 1, 1, 2]
K_PIECE = [0, 1, 2, 0, 1, 0]
TERMS = len(Q_PIECE)
ROW_ZERO = TERMS * D
ROW_PAGE = 64
ROW_MAX = P - 3
NPAGE = T // PAGE
MASKED = -3.0e38

UNITS = [
    [(0, 0, 0, 0, 512)],
    [(1, 0, 0, 0, 512)],
    [(0, 2, 0, 256, 256), (1, 6, 256, 256, 256)],
    [(0, 1, 0, 128, 384), (0, 3, 384, 384, 128)],
    [(1, 1, 0, 0, 512)],
    [(1, 2, 0, 0, 512)],
    [(1, 3, 0, 0, 512)],
    [(1, 4, 0, 0, 512)],
    [(1, 5, 0, 128, 384), (1, 7, 384, 384, 128)],
]
NU = len(UNITS)
FIRST_UNIT = [0, 1]
LAST_UNIT = [3, NU - 1]

BINS = [
    ([(0, 0), (4, 512)], 128, 0, 8),
    ([(1, 0), (5, 512)], 256, 1, 8),
    ([(2, 0)], 384, 2, 1),
    ([(6, 512)], 384, 10, 1),
    ([(3, 0)], 512, 3, 1),
    ([(4, 0)], 512, 4, 1),
    ([(5, 0)], 512, 5, 1),
    ([(6, 0)], 512, 6, 1),
    ([(7, 0)], 512, 7, 1),
    ([(7, 512)], 512, 11, 1),
]
GROUP_BINS = [(h, n) for h in range(HG) for n in range(len(BINS))]
NB = len(GROUP_BINS) + 1
LEAD = 3
PARTS = [GROUP_BINS[u * (NB - 1) // NU:(u + 1) * (NB - 1) // NU] for u in range(NU)]
BEFORE = [u * (NB - 1) // NU for u in range(NU)]



class Mem:

    def __init__(self, nc, stack):
        self.nc, self.stack = nc, stack

    def sb(self, name, shape, dt=F32):
        return self.stack.enter_context(self.nc.sbuf_tensor(name, shape, dt))

    def ps(self, name, shape, dt=F32):
        return self.stack.enter_context(self.nc.psum_tensor(name, shape, dt))

    def sem(self, name):
        return self.stack.enter_context(self.nc.semaphore(name))


def adaln_block(nc, w, out):
    with ExitStack() as stack:
        m = Mem(nc, stack)
        m.w, m.out = w, out
        m.qp = nc.dram_tensor("q_pieces", (3, GROUPS, HG * D, T), BF16).ap()
        m.kp = nc.dram_tensor("k_pieces", (3, GROUPS, HG * D, T), BF16).ap()
        m.x = m.sb("x_sb", [P, NT, E])
        m.ident = m.sb("ident", [P, P])
        m.identb = m.sb("identb", [P, P], BF16)
        m.modc = m.sb("modc", [P, 6, B])
        m.gbd = m.sb("gb_diag", [P, B, P])
        m.wog = m.sb("wog", [P, B, E])
        m.w1_hi = m.sb("w1_hi", [P, NE, FF], F32R)
        m.w1_lo = m.sb("w1_lo", [P, NE, FF], F32R)
        m.w2_hi = m.sb("w2_hi", [P, NE * FF // P, E], F32R)
        m.w2_lo = m.sb("w2_lo", [P, NE * FF // P, E], F32R)
        m.cur = m.sb("cur", [P, NCH, CH])
        m.mv = m.sb("mv", [P, NT, 2])
        m.stats = m.sb("stats", [P, NT, 6])
        m.ve = m.sb("ve", [P, NT, 1])
        m.sd = m.sb("sd", [P, NT, 1])
        m.rstd = m.sb("rstd", [P, NT, 1])
        m.nw = m.sb("nw", [P, NT, 1])
        m.wg = m.sb("wg_sb", [P, R + 1, NE])
        m.bg = m.sb("bg_sb", [P, R + 1, 1, NE])
        m.b1 = m.sb("b1_sb", [P, NE, FF // P])
        m.b2 = m.sb("b2_sb", [P, NE])
        m.tri = m.sb("tri", [P, 2, NE, NE])
        with ExitStack() as upto_attention:
            ma = Mem(nc, upto_attention)
            m.v = ma.sb("v_all", [P, GROUPS, JB, HG * D])
            m.ks = [ma.sb(f"ks{s}", [P, HG, T], BF16) for s in range(SLOTS)]
            m.qs = [ma.sb(f"qs{s}", [P, HG, T], BF16) for s in range(SLOTS)]
            m.qk_in = [ma.sem(f"qk_in{s}") for s in range(SLOTS)]
            with ExitStack() as part:
                prep(nc, m, Mem(nc, part))
            m.ovs = ma.sb("ovs", [P, GROUPS, 2, CH])
            with ExitStack() as part:
                attention(nc, m, Mem(nc, part))
            with ExitStack() as part:
                project(nc, m, Mem(nc, part))
        with ExitStack() as part:
            ffn(nc, m, Mem(nc, part))


def rstd_steps(nc, v, link, var_ok, sqrt_ok, m):
    nc.vector.tensor_scalar(m.ve[:, :, :], m.mv[:, :, 1:2], EPS, None, ALU.add).then_inc(var_ok, 1)
    v.wait_ge(sqrt_ok, 1)
    link(nc.vector.reciprocal(m.rstd[:, :, :], m.sd[:, :, :]))
    link(nc.vector.tensor_tensor(m.nw[:, :, :], m.rstd[:, :, :], m.rstd[:, :, :], ALU.mult))
    link(nc.vector.tensor_tensor(m.nw[:, :, :], m.nw[:, :, :], m.ve[:, :, :], ALU.mult))
    link(nc.vector.tensor_scalar(m.nw[:, :, :], m.nw[:, :, :], -0.5, 1.5, ALU.mult, ALU.add))
    link(nc.vector.tensor_tensor(m.rstd[:, :, :], m.rstd[:, :, :], m.nw[:, :, :], ALU.mult))


LOADS = [(0, 3), (3, 2), (5, 1)]


def load_group(sp, m, g, s):
    for first, n in LOADS:
        rows = slice(first * D, (first + n) * D)
        sp.dma_start(m.ks[s][rows, :, :],
                     m.kp[0:n, g].rearrange("c (d h) t -> c d (h t)", d=D)).then_inc(m.qk_in[s], 16)
        one = m.qp[Q_PIECE[first]:Q_PIECE[first] + 1, g].rearrange("c (d h) t -> c d (h t)", d=D)
        sp.dma_start(m.qs[s][rows, :, :], one.broadcast_to([n, D, HG * T])).then_inc(m.qk_in[s], 16)


def prep(nc, m, l):
    w = m.w
    ct, ce, sc = (l.sb(n, [P, B]) for n in ("ct", "ce", "sc"))
    wmod = l.sb("wmod", [P, 6 * E])
    wq, wqs = l.sb("wq", [E, E]), l.sb("wqs", [E, E])
    wd = l.sb("wd", [E, LAT])
    wk, wks = l.sb("wk", [LAT, E]), l.sb("wks", [LAT, E])
    wv = l.sb("wv", [LAT, E])
    wo = l.sb("wo", [E, E])
    cos, sin = l.sb("cos", [P, T]), l.sb("sin", [P, T])
    xn = l.sb("xn", [P, NT, E])
    lat = l.sb("lat", [LAT, 2, CH])
    ga = l.sb("ga", [P, B, E])
    gt, gs = l.sb("gt", [P, B, E]), l.sb("gs", [P, B, E])
    bt, bs = l.sb("bt", [P, B]), l.sb("bs", [P, B])
    rc = [l.sb(f"rc{s}", [P, CH]) for s in "qk"]
    rs = [l.sb(f"rs{s}", [P, CH]) for s in "qk"]
    ro = [l.sb(f"ro{s}", [P, 2, CH]) for s in "qk"]
    rr = [l.sb(f"rr{s}", [P, CH]) for s in "qk"]
    pieces = [l.sb(f"pieces_{s}", [P, NCH, 3, CH], BF16) for s in "qk"]
    turned = [l.ps(f"turned{i}", [P, CH]) for i in range(2)]
    pq = [l.ps(f"pq{i}", [P, CH]) for i in range(2)]
    pk = [l.ps(f"pk{i}", [P, CH]) for i in range(2)]
    plat = l.ps("plat", [P, CH])
    pmod = l.ps("pmod", [P, CH])

    in_c, in_mod, in_w, in_tab, in_rows = (l.sem(n) for n in ("in_c", "in_mod", "in_w", "in_tab", "in_rows"))
    in_x = [l.sem(f"in_x{c}") for c in range(NCH)]
    exp_c, silu_c, mods, mod_read = (l.sem(n) for n in ("exp_c", "silu_c", "mods", "mod_read"))
    var_ok, sqrt_ok, xn_ok, turn_ok, h_ok = (l.sem(n) for n in ("var_ok", "sqrt_ok", "xn_ok", "turn_ok", "h_ok"))
    swap_ok, q_ok, lat_ok, lat_sb, k_ok, v_ok, v_sb = (
        l.sem(n) for n in ("swap_ok", "q_ok", "lat_ok", "lat_sb", "k_ok", "v_ok", "v_sb"))
    rot, rot_read = l.sem("rot"), l.sem("rot_read")
    piece0, piece1, piece2, rest = (l.sem(n) for n in ("piece0", "piece1", "piece2", "rest"))
    dve, zeroed, pieces_out = l.sem("dve_prep"), l.sem("zeroed"), l.sem("pieces_out")

    with nc.Block() as block:

        @block.sync
        def _(sp):
            x_dram = w["x"].rearrange("b (t p) e -> p (b t) e", p=P)
            for c in range(NCH):
                sp.dma_start(m.x[:, TPC * c:TPC * (c + 1), :], x_dram[:, TPC * c:TPC * (c + 1), :]).then_inc(in_x[c], 16)
            for s in range(SLOTS):
                for rows, dst in ((w["k_rows"].bitcast(BF16), m.ks[s]), (w["q_rows"].bitcast(BF16), m.qs[s])):
                    n = rows.shape[0]
                    sp.dma_start(dst[ROW_ZERO:ROW_ZERO + n, :, :],
                                 rows.rearrange("r (h t) -> r h t", h=1).broadcast_to([n, HG, T])).then_inc(in_rows, 16)
            for c in range(NCH):
                b, at = c // 2, slice(CH * (c % 2), CH * (c % 2) + CH)
                for side, dst in enumerate((m.qp, m.kp)):
                    n = 2 * c + side + 1
                    sp.wait_ge(piece0, n)
                    sp.wait_ge(piece1, n)
                    sp.wait_ge(piece2, n)
                    sp.dma_start(dst.rearrange("c g r t -> (g r) c t")[b * P:(b + 1) * P, :, at],
                                 pieces[side][:, c, :, :]).then_inc(pieces_out, 16)
                if c == 1:
                    sp.wait_ge(pieces_out, 16 * 4)
                    load_group(sp, m, 0, 0)
                    load_group(sp, m, 1, 1)
            sp.wait_ge(in_rows, 16 * SLOTS * 2)
            sp.wait_ge(pieces_out, 16 * NCH * 2)

        @block.scalar
        def _(act):
            act.dma_start(ct[:, :], w["c"]).then_inc(in_c, 16)
            act.dma_start(wmod[:, :], w["wmod"]).then_inc(in_mod, 16)
            act.dma_start(m.ident[:, :], w["ident"]).then_inc(in_mod, 16)
            for dst, name in ((wq, "wq"), (wd, "w_down"), (wk, "wk_up"), (wv, "wv_up"), (wo, "wo")):
                act.dma_start(dst[:, :], w[name]).then_inc(in_w, 16)
            act.dma_start(cos[:, :], w["cos"]).then_inc(in_tab, 16)
            act.dma_start(sin[:, :], w["sin"]).then_inc(in_tab, 16)
            act.wait_ge(in_c, 16)
            nc.scalar.activation(ce[:, :], ct[:, :], ACT.Exp, scale=-1.0).then_inc(exp_c, 1)
            act.wait_ge(var_ok, 1)
            nc.scalar.activation(m.sd[:, :, :], m.ve[:, :, :], ACT.Sqrt).then_inc(sqrt_ok, 1)

            def hidden(c):
                b = c // 2
                act.wait_ge(turn_ok, c + 1)
                nc.scalar.activation(m.cur[:, c, :], turned[c % 2][:, :], ACT.Identity,
                                     bias=m.modc[:, 0, b:b + 1], scale=m.modc[:, 1, b:b + 1]).then_inc(h_ok, 1)

            def first_piece(c, side):
                act.wait_ge(rot, 2 * c + side + 1)
                nc.scalar.activation(pieces[side][:, c, 0, :], ro[side][:, c % 2, :], ACT.Copy).then_inc(piece0, 1)

            def second_piece(c, side):
                act.wait_ge(rest, 2 * c + side + 1)
                nc.scalar.activation(pieces[side][:, c, 1, :], rr[side][:, :], ACT.Copy).then_inc(piece1, 1)

            act.wait_ge(mod_read, 1)
            hidden(0)
            for c in range(NCH + 1):
                if c < NCH:
                    act.wait_ge(lat_ok, c + 1)
                    nc.scalar.activation(lat[:, c % 2, :], plat[0:LAT, :], ACT.Copy).then_inc(lat_sb, 1)
                if c + 1 < NCH:
                    hidden(c + 1)
                if c >= 1:
                    first_piece(c - 1, 0)
                    first_piece(c - 1, 1)
                    second_piece(c - 1, 0)
                    second_piece(c - 1, 1)
                if c < NCH:
                    b, j = c // 2, TPC * (c % 2)
                    act.wait_ge(v_ok, c + 1)
                    nc.scalar.activation(m.v[:, b * NG:(b + 1) * NG, j:j + TPC, :],
                                         pmod[:, :].rearrange("p (j g r) -> p g j r", j=TPC, g=NG),
                                         ACT.Copy).then_inc(v_sb, 1)

        @block.gpsimd
        def _(pool):
            for c in range(NCH):
                for side in range(2):
                    n = 2 * c + side
                    pool.wait_ge(piece0, n + 1)
                    if n >= 2:
                        pool.wait_ge(piece1, n - 1)
                        pool.wait_ge(piece2, n - 1)
                    nc.gpsimd.tensor_tensor(rr[side][:, :], ro[side][:, c % 2, :], pieces[side][:, c, 0, :],
                                            ALU.subtract).then_inc(rest, 1)
                for side in range(2):
                    n = 2 * c + side
                    pool.wait_ge(piece1, n + 1)
                    pool.wait_ge(rest, n + 1)
                    nc.gpsimd.tensor_tensor(pieces[side][:, c, 2, :], rr[side][:, :], pieces[side][:, c, 1, :],
                                            ALU.subtract).then_inc(piece2, 1)

        @block.vector
        def _(v):
            links = [0]

            def link(ins):
                links[0] += 1
                ins.then_inc(dve, 1)
                v.wait_ge(dve, links[0])

            for c in range(NCH):
                v.wait_ge(in_x[c], 16)
                for t in range(TPC * c, TPC * c + TPC):
                    s = nc.vector.bn_stats(m.stats[:, t, :], m.x[:, t, :])
                if c == 1:
                    v.wait_ge(exp_c, 1)
                    link(nc.vector.tensor_scalar(ce[:, :], ce[:, :], 1.0, None, ALU.add))
                    link(nc.vector.reciprocal(ce[:, :], ce[:, :]))
                    nc.vector.tensor_tensor(sc[:, :], ct[:, :], ce[:, :], ALU.mult).then_inc(silu_c, 1)
            link(s)
            for t in range(NT):
                s = nc.vector.bn_aggr(m.mv[:, t, :], m.stats[:, t, :])
            link(s)

            rstd_steps(nc, v, link, var_ok, sqrt_ok, m)
            v.wait_ge(mods, 1)
            link(nc.vector.tensor_copy(m.modc[:, :, :], pmod[:, 0:6 * B].rearrange("p (i b) -> p i b", b=B)))
            for i in (1, 4):
                s = nc.vector.tensor_scalar(m.modc[:, i, :], m.modc[:, i, :], 1.0, None, ALU.add)
            s.then_inc(mod_read, 1)
            for c in range(NCH):
                for t in range(TPC * c, TPC * c + TPC):
                    s = nc.vector.tensor_scalar(xn[:, t, :], m.x[:, t, :], m.mv[:, t, 0:1], m.rstd[:, t, :],
                                                ALU.subtract, ALU.mult)
                s.then_inc(xn_ok, 1)
                if c == 0:
                    v.wait_ge(in_w, 80)
                    for dst, src in ((wqs, wq), (wks, wk)):
                        pd, ps = (a[:, :].rearrange("p (i two h) -> p i two h", two=2, h=HG) for a in (dst, src))
                        nc.vector.tensor_scalar(pd[:, :, 0:1, :], ps[:, :, 1:2, :], -1.0, None, ALU.mult)
                        s = nc.vector.tensor_copy(pd[:, :, 1:2, :], ps[:, :, 0:1, :])
                    s.then_inc(swap_ok, 1)
                    nc.vector.tensor_copy(m.identb[:, :], m.ident[:, :])
                    nc.vector.tensor_copy(ga[:, :, :], pmod[:, E:E + B * E].rearrange("p (b e) -> p b e", b=B))\
                        .then_inc(mod_read, 1)
            v.wait_ge(in_tab, 32)
            for c in range(NCH):
                tab = slice(CH * (c % 2), CH * (c % 2) + CH)
                for side, (ready, pp) in enumerate(((q_ok, pq), (k_ok, pk))):
                    n = 2 * c + side
                    v.wait_ge(ready, c + 1)
                    nc.vector.tensor_tensor(rc[side][:, :], pp[0][:, :], cos[:, tab], ALU.mult)
                    s = nc.vector.tensor_tensor(rs[side][:, :], pp[1][:, :], sin[:, tab], ALU.mult)
                    s.then_inc(rot_read, 1)
                    v.wait_ge(rot_read, n + 1)
                    if c >= 2:
                        v.wait_ge(piece0, n - 3)
                        v.wait_ge(rest, n - 3)
                    nc.vector.tensor_tensor(ro[side][:, c % 2, :], rc[side][:, :], rs[side][:, :], ALU.add).then_inc(rot, 1)
            for g, t, s in ((ga[:, :, :], gt[:, :, :], gs[:, :, :]), (m.modc[:, 5, :], bt[:, :], bs[:, :])):
                link(nc.vector.tensor_scalar(t, g, -1.0, None, ALU.mult))
                link(nc.vector.tensor_tensor(t, t, g, ALU.max))
                link(nc.vector.tensor_scalar(t, t, 0.25, None, ALU.max))
                link(nc.vector.tensor_scalar(s, g, 0.0, 2.0, ALU.is_ge, ALU.mult))
                link(nc.vector.tensor_scalar(s, s, -1.0, None, ALU.add))
                link(nc.vector.tensor_tensor(t, t, s, ALU.mult))
            for b in range(B):
                nc.vector.tensor_tensor(m.wog[:, b, :], wo[:, :], gt[:, b, :], ALU.mult)
                nc.vector.tensor_scalar(m.gbd[:, b, :], m.ident[:, :], bt[:, b:b + 1], None, ALU.mult)

        @block.tensor
        def _(pe):
            pe.wait_ge(silu_c, 1)
            pe.wait_ge(in_mod, 32)
            for i in range(6):
                nc.tensor.matmul(pmod[:, i * B:(i + 1) * B], wmod[:, i * E:(i + 1) * E], sc[:, :], start=True, stop=True)
            for b in range(B):
                mm = nc.tensor.matmul(pmod[:, E + b * E:E + (b + 1) * E], sc[:, b:b + 1].broadcast_to([P, P]),
                                      wmod[:, 2 * E:3 * E], start=True, stop=True)
            mm.then_inc(mods, 1)

            def turn(c):
                pe.wait_ge(xn_ok, c + 1)
                if c >= 2:
                    pe.wait_ge(h_ok, c - 1)
                for i in range(TPC):
                    mm = nc.tensor.transpose(turned[c % 2][:, i * P:(i + 1) * P], xn[:, TPC * c + i, :], m.ident[:, :])
                mm.then_inc(turn_ok, 1)

            turn(0)
            pe.wait_ge(swap_ok, 1)
            for c in range(NCH):
                pe.wait_ge(h_ok, c + 1)
                if c >= 1:
                    pe.wait_ge(lat_sb, c)
                nc.tensor.matmul(plat[0:LAT, :], wd[:, :], m.cur[:, c, :], start=True, stop=True).then_inc(lat_ok, 1)
                if c + 1 < NCH:
                    turn(c + 1)
                if c >= 1:
                    pe.wait_ge(rot_read, 2 * c)
                nc.tensor.matmul(pq[0][:, :], wq[:, :], m.cur[:, c, :], start=True, stop=True)
                nc.tensor.matmul(pq[1][:, :], wqs[:, :], m.cur[:, c, :], start=True, stop=True).then_inc(q_ok, 1)
                pe.wait_ge(lat_sb, c + 1)
                nc.tensor.matmul(pk[0][:, :], wk[:, :], lat[:, c % 2, :], start=True, stop=True)
                nc.tensor.matmul(pk[1][:, :], wks[:, :], lat[:, c % 2, :], start=True, stop=True).then_inc(k_ok, 1)
                if c == 0:
                    pe.wait_ge(mod_read, 2)
                if c >= 1:
                    pe.wait_ge(v_sb, c)
                for i in range(TPC):
                    mm = nc.tensor.matmul(pmod[:, i * P:(i + 1) * P], lat[:, c % 2, i * P:(i + 1) * P], wv[:, :],
                                          start=True, stop=True)
                mm.then_inc(v_ok, 1)


def attention(nc, m, l):
    probs = [l.sb(f"probs{s}", [P, HG, CH]) for s in range(SLOTS)]
    vs = [l.sb(f"vs{s}", [P, JB, HG, 32]) for s in range(SLOTS)]
    mcol = l.sb("mcol", [P, HG, 12])
    mres = l.sb("mres", [P, HG, JB])
    mpc = l.sb("mpc", [P, 3, HG, JB], BF16)
    mrow = l.sb("mrow", [3 * HG * JB, P], BF16)
    w1_raw = l.sb("w1_raw", [P, NE, FF])
    w2_raw = l.sb("w2_raw", [P, NE * FF // P, E])
    st = l.ps("st", [P, HG, CH])
    ov = l.ps("ov", [P, 2, CH])
    mx = l.ps("mx", [P, 2, CH])

    qk_in = m.qk_in
    mrow_in = [l.sem(f"mrow_in{s}") for s in range(SLOTS)]
    st_done, exp_done, pv_done, ov_read = (l.sem(n) for n in ("st_done", "exp_done", "pv_done", "ov_read"))
    bin_full, bin_read, mchain = (l.sem(n) for n in ("bin_full", "bin_read", "mchain"))
    vs_init, vs_ok, w_in, w_hi, w_lo, small_in = (
        l.sem(n) for n in ("vs_init", "vs_ok", "w_in", "w_hi", "w_lo", "small_in"))
    ST_CREDIT, EXP_CREDIT, PV_CREDIT, OV_CREDIT = 1, 2, SLOTS, 2
    CHAIN = 6

    def gnum(i, a):
        return SLOTS * i + a

    def exists(i, a):
        return not isinstance(i, int) or SLOTS * i + a < GROUPS

    def uses(i, a):
        return i + (a // SLOTS + 1)

    def all_groups(eng, body):
        whole = (GROUPS - 2) // SLOTS
        with eng.Fori(0, whole) as i:
            for a in range(SLOTS):
                body(i, a)
        for g in range(whole * SLOTS, GROUPS):
            body(whole, g - whole * SLOTS)

    def following(i, a, u):
        return (i, a, u + 1) if u + 1 < NU else (i, a + 1, 0)

    def part_at(i, a, u):
        n = u + LEAD
        return (i, a + 1, n) if n < NU else (i, a + 2, n - NU)

    with nc.Block() as block:

        @block.sync
        def _(sp):
            def max_rows(i, a):
                s = a % SLOTS
                sp.wait_ge(bin_read, NB * gnum(i, a) + NB)
                sp.dma_start(m.qs[s][ROW_MAX:ROW_MAX + 3, :, :], mrow[:, :]).then_inc(mrow_in[s], 16)

            def body(i, a):
                if exists(i, a + 2):
                    sp.wait_ge(st_done, 2 * NU * gnum(i, a) + ST_CREDIT)
                    load_group(sp, m, gnum(i, a + 2), (a + 2) % SLOTS)
                if exists(i, a + 1):
                    max_rows(i, a + 1)

            max_rows(0, 0)
            sp.dma_start(w1_raw[:, :, :], m.w["W1"].rearrange("e h f -> h e f")).then_inc(w_in, 16)
            sp.dma_start(w2_raw[:, :, :], m.w["W2"].rearrange("e (c f) h -> f (e c) h", f=P)).then_inc(w_in, 16)
            sp.dma_start(m.wg[:, 0:R, :], m.w["Wg"]).then_inc(small_in, 16)
            sp.dma_start(m.wg[:, R:R + 1, :], m.w["Wg"][:, R - 1:R, :]).then_inc(small_in, 16)
            sp.dma_start(m.bg[:, 0:R, :, :], m.w["bg"]).then_inc(small_in, 16)
            sp.dma_start(m.bg[:, R:R + 1, :, :], m.w["bg"][:, R - 1:R, :, :]).then_inc(small_in, 16)
            sp.dma_start(m.b1[:, :, :], m.w["b1"]).then_inc(small_in, 16)
            sp.dma_start(m.b2[:, :], m.w["b2"]).then_inc(small_in, 16)
            sp.dma_start(m.tri[:, :, :, :], m.w["tri"]).then_inc(small_in, 16)
            all_groups(sp, body)
            sp.wait_ge(small_in, 112)

        @block.gpsimd
        def _(pool):
            def stage(i, a):
                s = a % SLOTS
                nc.gpsimd.tensor_copy(vs[s][:, :, :, 0:D],
                                      m.v[:, gnum(i, a), :, :].rearrange("p j (h d) -> p j h d", d=D)).then_inc(vs_ok, 1)

            for s in range(SLOTS):
                nc.gpsimd.memset(vs[s][:, :, :, :], 0.0).then_inc(vs_init, 1)
            pool.wait_ge(vs_init, SLOTS)
            for s in range(SLOTS):
                nc.gpsimd.memset(vs[s][:, :, :, D:D + 1], 1.0).then_inc(vs_init, 1)
            pool.wait_ge(vs_init, 2 * SLOTS)
            stage(0, 0)
            stage(0, 1)
            pool.wait_ge(w_in, 32)
            for e in range(NE):
                c = slice(e * FF // P, (e + 1) * FF // P)
                nc.gpsimd.tensor_copy(m.w1_hi[:, e, :], w1_raw[:, e, :])
                nc.gpsimd.tensor_copy(m.w2_hi[:, c, :], w2_raw[:, c, :]).then_inc(w_hi, 1)
                pool.wait_ge(w_hi, e + 1)
                nc.gpsimd.tensor_tensor(m.w1_lo[:, e, :], w1_raw[:, e, :], m.w1_hi[:, e, :], ALU.subtract)
                nc.gpsimd.tensor_tensor(m.w2_lo[:, c, :], w2_raw[:, c, :], m.w2_hi[:, c, :],
                                        ALU.subtract).then_inc(w_lo, 1)

            def body(i, a):
                if exists(i, a + 2):
                    pool.wait_ge(vs_init, 2 * SLOTS)
                    pool.wait_ge(pv_done, NU * gnum(i, a) + PV_CREDIT)
                    stage(i, a + 2)

            all_groups(pool, body)

        @block.scalar
        def _(act):
            def exps(i, a, u):
                n = NU * gnum(i, a) + u
                for half in range(2):
                    h = slice(2 * half, 2 * half + 2)
                    act.wait_ge(st_done, 2 * n + half + 1 + ST_CREDIT)
                    if half == 0:
                        act.wait_ge(pv_done, n + 1 - SLOTS + PV_CREDIT)
                    nc.scalar.activation(probs[u % SLOTS][:, h, :], st[:, h, :], ACT.Exp,
                                         scale=SCALE).then_inc(exp_done, 1)

            def keep_output(i, a, c):
                g = gnum(i, a)
                act.wait_ge(pv_done, NU * g + LAST_UNIT[c] + 1 + PV_CREDIT)
                nc.scalar.activation(m.ovs[:, g, c, :], ov[:, c, :], ACT.Copy).then_inc(ov_read, 1)

            def body(i, a):
                for u in range(NU):
                    if exists(*following(i, a, u)[:2]):
                        exps(*following(i, a, u))
                    if u == LAST_UNIT[0] + 1:
                        keep_output(i, a, 0)
                keep_output(i, a, 1)

            exps(0, 0, 0)
            all_groups(act, body)

        @block.vector
        def _(v):
            def read_bin(i, a, k):
                h, b = GROUP_BINS[k]
                blocks, keys, slot, step = BINS[b]
                n = NB * gnum(i, a) + k
                v.wait_ge(bin_full, n + 1)
                nc.vector.tensor_reduce(mcol[:, h, slot:slot + step * (len(blocks) - 1) + 1:step],
                                        mx[:, k % 2, 0:len(blocks) * keys].rearrange("p (b k) -> p b k", k=keys),
                                        AX.X, ALU.max, negate=True).then_inc(bin_read, 1)

            def maxima(i, a):
                g = gnum(i, a)
                at = [CHAIN * g]

                def link(ins):
                    at[0] = at[0] + 1
                    ins.then_inc(mchain, 1)
                    v.wait_ge(mchain, at[0])

                v.wait_ge(bin_read, NB * g + NB - 1)
                nm = mcol[:, :, 0:JB]
                link(nc.vector.tensor_tensor(mcol[:, :, 4:8], mcol[:, :, 4:8], mcol[:, :, 8:12], ALU.min))
                link(nc.vector.tensor_copy(mpc[:, 0, :, :], nm))
                link(nc.vector.tensor_tensor(mres[:, :, :], nm, mpc[:, 0, :, :], ALU.subtract))
                link(nc.vector.tensor_copy(mpc[:, 1, :, :], mres[:, :, :]))
                link(nc.vector.tensor_tensor(mres[:, :, :], mres[:, :, :], mpc[:, 1, :, :], ALU.subtract))
                link(nc.vector.tensor_copy(mpc[:, 2, :, :], mres[:, :, :]))
                v.wait_ge(bin_full, NB * g + NB)
                if not isinstance(i, int) or SLOTS * i + a > 0:
                    s = (a - 1) % SLOTS
                    v.wait_ge(mrow_in[s], 16 * uses(i, a - 1))
                nc.vector.tensor_copy(mrow[:, :], mx[0:3 * HG * JB, (NB - 1) % 2, 0:P // 2].bitcast(BF16))\
                    .then_inc(bin_read, 1)

            def part(i, a, p):
                for k in range(BEFORE[p], BEFORE[p] + len(PARTS[p])):
                    read_bin(i, a, k)
                if p == NU - 1:
                    maxima(i, a)

            def body(i, a):
                for u in range(NU):
                    if exists(*part_at(i, a, u)[:2]):
                        part(*part_at(i, a, u))

            for p in range(NU):
                part(0, 0, p)
            for p in range(LEAD):
                part(0, 1, p)
            all_groups(v, body)

        @block.tensor
        def _(pe):
            def scores(i, a, u, half):
                s, n = a % SLOTS, NU * gnum(i, a) + u
                if u == 0 and half == 0:
                    pe.wait_ge(qk_in[s], 16 * 2 * len(LOADS) * uses(i, a))
                    pe.wait_ge(mrow_in[s], 16 * uses(i, a))
                pe.wait_ge(exp_done, 2 * n - 1 + half + EXP_CREDIT)
                for h in (2 * half, 2 * half + 1):
                    for c, j, off, q0, nq in UNITS[u]:
                        mm = nc.tensor.matmul(st[:, h, off:off + nq], m.ks[s][:, h, j * P:(j + 1) * P],
                                              m.qs[s][:, h, c * CH + q0:c * CH + q0 + nq], start=True, stop=True)
                mm.then_inc(st_done, 1)

            def weigh(i, a, u):
                s, g = a % SLOTS, gnum(i, a)
                pe.wait_ge(exp_done, 2 * (NU * g + u + 1) + EXP_CREDIT)
                if u == FIRST_UNIT[0]:
                    pe.wait_ge(vs_ok, g + 1)
                for c in range(2):
                    if u == FIRST_UNIT[c]:
                        pe.wait_ge(ov_read, 2 * g - 1 + c + OV_CREDIT)
                for c, j, off, q0, nq in UNITS[u]:
                    for h in range(HG):
                        mm = nc.tensor.matmul(ov[32 * h:32 * h + 32, c, q0:q0 + nq], vs[s][:, j, h, :],
                                              probs[u % SLOTS][:, h, off:off + nq],
                                              start=(u == FIRST_UNIT[c]), stop=(u == LAST_UNIT[c]),
                                              skip_group_check=True)
                mm.then_inc(pv_done, 1)

            def fill_bin(i, a, k):
                s, n = a % SLOTS, NB * gnum(i, a) + k
                h, b = GROUP_BINS[k]
                if k == 0:
                    pe.wait_ge(qk_in[s], 16 * 2 * len(LOADS) * uses(i, a))
                if not isinstance(n, int) or n >= 2:
                    pe.wait_ge(bin_read, n if k == 0 else n - 1)
                blocks, keys, _, _ = BINS[b]
                for x, (t, k0) in enumerate(blocks):
                    mm = nc.tensor.matmul(mx[:, k % 2, x * keys:(x + 1) * keys],
                                          m.qs[s][0:ROW_MAX, h, t * P:(t + 1) * P],
                                          m.ks[s][0:ROW_MAX, h, k0:k0 + keys], start=True, stop=True)
                mm.then_inc(bin_full, 1)

            def turn_maxima(i, a):
                g = gnum(i, a)
                pe.wait_ge(mchain, CHAIN * g + CHAIN)
                pe.wait_ge(bin_read, NB * g + NB - 2)
                nc.tensor.transpose(mx[0:3 * HG * JB, (NB - 1) % 2, 0:P // 2].bitcast(BF16),
                                    mpc[:, :, :, :].rearrange("p c h t -> p (c h t)"),
                                    m.identb[:, :]).then_inc(bin_full, 1)

            def part(i, a, p, half):
                ks = range(BEFORE[p], BEFORE[p] + len(PARTS[p]))
                cut = len(PARTS[p]) // 2
                for k in (ks[:cut] if half == 0 else ks[cut:]):
                    fill_bin(i, a, k)

            def body(i, a):
                for u in range(NU):
                    nxt, side = following(i, a, u), part_at(i, a, u)
                    if side[2] == 0 and exists(i, a + 1):
                        turn_maxima(i, a + 1)
                    for half in range(2):
                        if exists(*nxt[:2]):
                            scores(*nxt, half)
                        if exists(*side[:2]):
                            part(*side, half)
                    weigh(i, a, u)

            nc.tensor.sem_inc(st_done, ST_CREDIT)
            nc.tensor.sem_inc(exp_done, EXP_CREDIT)
            nc.tensor.sem_inc(pv_done, PV_CREDIT)
            nc.tensor.sem_inc(ov_read, OV_CREDIT)
            for p in range(NU):
                part(0, 0, p, 0)
                part(0, 0, p, 1)
            turn_maxima(0, 0)
            for p in range(LEAD):
                part(0, 1, p, 0)
                part(0, 1, p, 1)
            scores(0, 0, 0, 0)
            scores(0, 0, 0, 1)
            all_groups(pe, body)


def project(nc, m, l):
    rec = l.sb("rec", [P, 2, NH, 1])
    att = l.sb("att", [P, 2, NH, D])
    att_t = l.sb("att_t", [P, 2, P])
    xn = l.sb("xn2", [P, NT, E])
    heads = [l.ps(f"heads{i}", [P, CH]) for i in range(2)]
    turn = [l.ps(f"turn{i}", [P, CH]) for i in range(2)]
    added = [l.ps(f"added{i}", [P, CH]) for i in range(2)]
    h_t = [l.ps(f"h_t{i}", [P, CH]) for i in range(2)]
    heads_ok, rec_ok, att_ok, turn_ok, att_sb, add_ok, x_ok = (
        l.sem(n) for n in ("heads_ok", "rec_ok", "att_ok", "turn2_ok", "att_sb", "add_ok", "x_ok"))
    dve, var_ok, sqrt_ok, xn_ok, ht_ok, h_ok = (
        l.sem(n) for n in ("dve_proj", "var2_ok", "sqrt2_ok", "xn2_ok", "ht_ok", "h2_ok"))

    with nc.Block() as block:

        @block.tensor
        def _(pe):
            def to_tokens(t):
                if t >= 2:
                    pe.wait_ge(att_ok, t - 1)
                b, c, i = t // JB, t % JB // TPC, t % TPC
                for hg in range(NG):
                    mm = nc.tensor.transpose(heads[t % 2][:, hg * P:(hg + 1) * P],
                                             m.ovs[:, b * NG + hg, c, i * P:(i + 1) * P], m.ident[:, :])
                mm.then_inc(heads_ok, 1)

            def back(t):
                pe.wait_ge(att_ok, t + 1)
                if t >= 2:
                    pe.wait_ge(att_sb, t - 1)
                nc.tensor.transpose(turn[t % 2][:, 0:P], att[:, t % 2, :, :].rearrange("p h d -> p (h d)"),
                                    m.ident[:, :]).then_inc(turn_ok, 1)

            def wo(t):
                pe.wait_ge(att_sb, t + 1)
                if t >= 2:
                    pe.wait_ge(x_ok, t - 1)
                nc.tensor.matmul(added[t % 2][:, 0:E], att_t[:, t % 2, :], m.wog[:, t // JB, :],
                                 start=True, stop=True).then_inc(add_ok, 1)

            for t in range(NT + 2):
                if t < NT:
                    to_tokens(t)
                if 1 <= t <= NT:
                    back(t - 1)
                if t >= 2:
                    wo(t - 2)
            for c in range(NCH):
                pe.wait_ge(xn_ok, c + 1)
                if c >= 2:
                    pe.wait_ge(h_ok, c - 1)
                for i in range(TPC):
                    mm = nc.tensor.transpose(h_t[c % 2][:, i * P:(i + 1) * P], xn[:, TPC * c + i, :], m.ident[:, :])
                mm.then_inc(ht_ok, 1)

        @block.scalar
        def _(act):
            for t in range(NT):
                act.wait_ge(turn_ok, t + 1)
                if t >= 2:
                    act.wait_ge(add_ok, t - 1)
                nc.scalar.activation(att_t[:, t % 2, :], turn[t % 2][:, 0:P], ACT.Copy).then_inc(att_sb, 1)
            act.wait_ge(var_ok, 1)
            nc.scalar.activation(m.sd[:, :, :], m.ve[:, :, :], ACT.Sqrt).then_inc(sqrt_ok, 1)
            for c in range(NCH):
                b = c // 2
                act.wait_ge(ht_ok, c + 1)
                nc.scalar.activation(m.cur[:, c, :], h_t[c % 2][:, :], ACT.Identity,
                                     bias=m.modc[:, 3, b:b + 1], scale=m.modc[:, 4, b:b + 1]).then_inc(h_ok, 1)

        @block.vector
        def _(v):
            links = [0]

            def link(ins):
                links[0] += 1
                ins.then_inc(dve, 1)
                v.wait_ge(dve, links[0])

            def divide(t):
                v.wait_ge(heads_ok, t + 1)
                if t >= 2:
                    v.wait_ge(turn_ok, t - 1)
                o = heads[t % 2][:, :].rearrange("p (h r) -> p h r", r=32)
                nc.vector.reciprocal(rec[:, t % 2, :, :], o[:, :, D:D + 1]).then_inc(rec_ok, 1)
                v.wait_ge(rec_ok, t + 1)
                nc.vector.tensor_tensor(att[:, t % 2, :, :], o[:, :, 0:D],
                                        rec[:, t % 2, :, :].broadcast_to([P, NH, D]), ALU.mult).then_inc(att_ok, 1)

            def residual(t):
                v.wait_ge(add_ok, t + 1)
                nc.vector.tensor_tensor(m.x[:, t, :], m.x[:, t, :], added[t % 2][:, 0:E], ALU.add).then_inc(x_ok, 1)
                v.wait_ge(x_ok, t + 1)
                return nc.vector.bn_stats(m.stats[:, t, :], m.x[:, t, :])

            for t in range(NT + 2):
                if t < NT:
                    divide(t)
                if t >= 2:
                    last = residual(t - 2)
            link(last)
            for t in range(NT):
                last = nc.vector.bn_aggr(m.mv[:, t, :], m.stats[:, t, :])
            link(last)
            rstd_steps(nc, v, link, var_ok, sqrt_ok, m)
            for c in range(NCH):
                for t in range(TPC * c, TPC * c + TPC):
                    last = nc.vector.tensor_scalar(xn[:, t, :], m.x[:, t, :], m.mv[:, t, 0:1], m.rstd[:, t, :],
                                                   ALU.subtract, ALU.mult)
                last.then_inc(xn_ok, 1)


def ffn(nc, m, l):
    K = NE * FF // P
    NS = NCH * K
    AHEAD, RING = 3, 4
    cur_hi = l.sb("cur_hi", [P, NCH, CH], F32R)
    cur_lo = l.sb("cur_lo", [P, NCH, CH], F32R)
    gel = [l.sb(f"gel{i}", [P, CH]) for i in range(RING)]
    gel_hi = [l.sb(f"gel_hi{i}", [P, CH], F32R) for i in range(RING)]
    gel_lo = [l.sb(f"gel_lo{i}", [P, CH], F32R) for i in range(RING)]
    cwb = l.sb("cwb", [P, NE, CH])
    part = l.sb("part", [P, 2, CH])
    log = l.sb("log", [P, TPC, NE])
    ge, gt = l.sb("at_least", [P, TPC, NE, NE]), l.sb("above", [P, TPC, NE, NE])
    rank, half, hdiff, dl = (l.sb(n, [P, TPC, NE]) for n in ("rank", "half", "hdiff", "dl"))
    gap, th = l.sb("gap", [P, TPC, 1]), l.sb("th", [P, TPC, 1])
    cw = l.sb("cw", [P, TPC, NE])
    hid = [l.ps(f"hid{i}", [P, CH]) for i in range(RING)]
    y = [l.ps(f"y{i}", [P, CH]) for i in range(2)]
    plog = l.ps("plog", [P, CH])
    pcw = l.ps("pcw", [P, CH])

    cur_ok, hi_ok, hid_ok, gel_ok, lo_ok, y_ok = (
        l.sem(n) for n in ("cur_ok", "hi_ok", "hid_ok", "gel_ok", "lo_ok", "y_ok"))
    log_ok, gap_ok, th_ok, cw_ok, pcw_ok, cwb_ok, part_ok, add_ok, chain = (
        l.sem(n) for n in ("log_ok", "gap_ok", "th_ok", "cw_ok", "pcw_ok", "cwb_ok", "part_ok", "addf_ok", "chain"))
    last_ok, out_ok, stored = (l.sem(n) for n in ("last_ok", "out_ok", "stored"))
    GEL_CREDIT, Y_CREDIT, PART_CREDIT, ADD_CREDIT, CWB_CREDIT = RING, RING, 2, 2, 1
    LINKS = 10

    def wrap(r, s):
        return (r + 1, s - NS) if s >= NS else (r, s)

    def split_step(s):
        return s // K, s % K // (FF // P), s % (FF // P)

    LOGITS, RANKS, TANH, WEIGHTS = [-14], [-13, -11, -10, -9], [-8], [-7]
    SPREAD = [-6 + 3 * e for e in range(NE)]
    KEEP = [-4 + 3 * e for e in range(NE)]

    def due(steps, s):
        return [(c, x) for c in range(NCH + 1) for x, at in enumerate(steps) if K * c + at == s]

    def before(steps):
        return [x for x, at in enumerate(steps) if at < 0]

    with nc.Block() as block:

        @block.tensor
        def _(pe):
            def up(r, s):
                r, s = wrap(r, s)
                c, e, q = split_step(s)
                if s % K == 0:
                    pe.wait_ge(cur_ok, NCH * r + c + 1)
                pe.wait_ge(gel_ok, NS * r + s - RING + 1 + GEL_CREDIT)
                f = slice(q * P, (q + 1) * P)
                h = hid[s % RING][:, :]
                nc.tensor.matmul(h, m.w1_hi[:, e, f], cur_hi[:, c, :], start=True, stop=False)
                nc.tensor.matmul(h, m.w1_hi[:, e, f], cur_lo[:, c, :], start=False, stop=False)
                nc.tensor.matmul(h, m.w1_lo[:, e, f], cur_hi[:, c, :], start=False, stop=True).then_inc(hid_ok, 1)

            def down(r, s):
                c, e, q = split_step(s)
                n = NE * (NCH * r + c) + e
                if q == 0:
                    pe.wait_ge(part_ok, n - 1 + PART_CREDIT)
                pe.wait_ge(lo_ok, NS * r + s + 1)
                o, x, first, last = y[e % 2][:, :], e * (FF // P) + q, q == 0, q == FF // P - 1
                nc.tensor.matmul(o, m.w2_hi[:, x, :], gel_hi[s % RING][:, :], start=first, stop=False)
                nc.tensor.matmul(o, m.w2_lo[:, x, :], gel_hi[s % RING][:, :], start=False, stop=False)
                nc.tensor.matmul(o, m.w2_hi[:, x, :], gel_lo[s % RING][:, :], start=False, stop=last).then_inc(y_ok, 1)

            def logits(r, c):
                pe.wait_ge(cur_ok, NCH * r + c + 1)
                for i in range(TPC):
                    mm = nc.tensor.matmul(plog[:, i * NE:(i + 1) * NE], m.cur[:, c % NCH, i * P:(i + 1) * P],
                                          m.wg[:, r + c // NCH, :], start=True, stop=True)
                mm.then_inc(log_ok, 1)

            def spread(r, c, e):
                n = NE * (NCH * r + c) + e
                pe.wait_ge(cw_ok, NCH * r + c + 1)
                pe.wait_ge(cwb_ok, n + CWB_CREDIT)
                for i in range(TPC):
                    mm = nc.tensor.transpose(pcw[:, i * P:(i + 1) * P], cw[:, i, e:e + 1].broadcast_to([P, P]),
                                             m.ident[:, :])
                mm.then_inc(pcw_ok, 1)

            nc.tensor.sem_inc(gel_ok, GEL_CREDIT)
            nc.tensor.sem_inc(y_ok, Y_CREDIT)
            nc.tensor.sem_inc(part_ok, PART_CREDIT)
            nc.tensor.sem_inc(add_ok, ADD_CREDIT)
            nc.tensor.sem_inc(cwb_ok, CWB_CREDIT)
            for s in range(AHEAD):
                up(0, s)
            logits(0, 0)
            for e in before(SPREAD):
                spread(0, 0, e)
            with pe.Fori(0, R) as r:
                for s in range(NS):
                    up(r, s + AHEAD)
                    for c, _ in due(LOGITS, s):
                        logits(r, c)
                    for c, e in due(SPREAD, s):
                        spread(r, c, e)
                    down(r, s)
            for c in range(NCH):
                pe.wait_ge(cur_ok, NCH * R + c + 1)
                if c == 0:
                    pe.wait_ge(gel_ok, NS * R + 1 + GEL_CREDIT)
                for i in range(TPC):
                    mm = nc.tensor.matmul(hid[(c + 3) % RING][:, i * P:(i + 1) * P], m.cur[:, c, i * P:(i + 1) * P],
                                          m.gbd[:, c // 2, :], start=True, stop=True)
                mm.then_inc(last_ok, 1)

        @block.scalar
        def _(act):
            def gelu(r, s):
                r, s = wrap(r, s)
                c, e, q = split_step(s)
                act.wait_ge(hid_ok, NS * r + s + 1)
                act.wait_ge(y_ok, NS * r + s - RING + 1 + Y_CREDIT)
                bias = m.b1[:, e, q:q + 1]
                nc.scalar.activation(gel[s % RING][:, :], hid[s % RING][:, :], ACT.Gelu_apprx_tanh, bias=bias)
                nc.scalar.activation(gel_hi[s % RING][:, :], hid[s % RING][:, :], ACT.Gelu_apprx_tanh,
                                     bias=bias).then_inc(gel_ok, 1)

            def keep(r, c, e):
                n = NE * (NCH * r + c) + e
                act.wait_ge(pcw_ok, n + 1)
                nc.scalar.activation(cwb[:, e, :], pcw[:, :], ACT.Copy).then_inc(cwb_ok, 1)

            def tanh(r, c):
                act.wait_ge(gap_ok, NCH * r + c + 1)
                nc.scalar.activation(th[:, :, :], gap[:, :, :], ACT.Tanh).then_inc(th_ok, 1)

            gelu(0, 0)
            tanh(0, 0)
            for e in before(KEEP):
                keep(0, 0, e)
            with act.Fori(0, R) as r:
                for s in range(NS):
                    gelu(r, s + 1)
                    for c, _ in due(TANH, s):
                        tanh(r, c)
                    for c, e in due(KEEP, s):
                        keep(r, c, e)

        @block.vector
        def _(v):
            def low(r, s):
                r, s = wrap(r, s)
                v.wait_ge(gel_ok, NS * r + s + 1 + GEL_CREDIT)
                nc.vector.tensor_tensor(gel_lo[s % RING][:, :], gel[s % RING][:, :], gel_hi[s % RING][:, :],
                                        ALU.subtract).then_inc(lo_ok, 1)

            def linker(r, c, at):
                at = [at]

                def link(ins):
                    at[0] += 1
                    ins.then_inc(chain, 1)
                    v.wait_ge(chain, LINKS * (NCH * r + c) + at[0])
                return link

            def ranks(r, c, stage):
                link = linker(r, c, [0, 3, 5, 7][stage])
                if stage == 0:
                    v.wait_ge(log_ok, NCH * r + c + 1)
                    link(nc.vector.tensor_tensor(log[:, :, :], plog[:, 0:TPC * NE].rearrange("p (t e) -> p t e", e=NE),
                                                 m.bg[:, r + c // NCH, :, :].broadcast_to([P, TPC, NE]), ALU.add))
                    other = log[:, :, :].rearrange("p t (e j) -> p t e j", e=1).broadcast_to([P, TPC, NE, NE])
                    own = log[:, :, :].rearrange("p t (e j) -> p t e j", j=1).broadcast_to([P, TPC, NE, NE])
                    link(nc.vector.tensor_tensor(ge[:, :, :, :], other, own, ALU.is_ge))
                    link(nc.vector.tensor_tensor(gt[:, :, :, :], other, own, ALU.is_gt))
                if stage == 1:
                    tri = [m.tri[:, i:i + 1, :, :].broadcast_to([P, TPC, NE, NE]) for i in range(2)]
                    nc.vector.tensor_tensor(ge[:, :, :, :], ge[:, :, :, :], tri[0], ALU.mult)
                    link(nc.vector.tensor_tensor(gt[:, :, :, :], gt[:, :, :, :], tri[1], ALU.mult))
                    link(nc.vector.tensor_tensor(ge[:, :, :, :], ge[:, :, :, :], gt[:, :, :, :], ALU.add))
                if stage == 2:
                    link(nc.vector.tensor_reduce(rank[:, :, :], ge[:, :, :, :], AX.X, ALU.add))
                    nc.vector.tensor_scalar(half[:, :, :], rank[:, :, :], 1.5, 0.5, ALU.is_lt, ALU.mult)
                    link(nc.vector.tensor_scalar(hdiff[:, :, :], rank[:, :, :], 0.5, None, ALU.is_lt))
                if stage == 3:
                    link(nc.vector.tensor_tensor(hdiff[:, :, :], hdiff[:, :, :], half[:, :, :], ALU.subtract))
                    link(nc.vector.tensor_tensor(dl[:, :, :], hdiff[:, :, :], log[:, :, :], ALU.mult))
                    nc.vector.tensor_reduce(gap[:, :, :], dl[:, :, :], AX.X, ALU.add).then_inc(gap_ok, 1)

            def weights(r, c):
                link = linker(r, c, LINKS - 1)
                v.wait_ge(th_ok, NCH * r + c + 1)
                link(nc.vector.tensor_tensor(cw[:, :, :], hdiff[:, :, :], th[:, :, :].broadcast_to([P, TPC, NE]),
                                             ALU.mult))
                nc.vector.tensor_tensor(cw[:, :, :], cw[:, :, :], half[:, :, :], ALU.add).then_inc(cw_ok, 1)

            def combine(r, c, e):
                n = NE * (NCH * r + c) + e
                v.wait_ge(y_ok, NS * r + K * c + (e + 1) * (FF // P) + Y_CREDIT)
                v.wait_ge(cwb_ok, n + 1 + CWB_CREDIT)
                v.wait_ge(add_ok, n - 1 + ADD_CREDIT)
                nc.vector.scalar_tensor_tensor(out=part[:, e % 2, :], in0=y[e % 2][:, :], scalar=m.b2[:, e:e + 1],
                                               in1=cwb[:, e, :], op0=ALU.add, op1=ALU.mult).then_inc(part_ok, 1)

            low(0, 0)
            for stage in range(len(RANKS)):
                ranks(0, 0, stage)
            weights(0, 0)
            with v.Fori(0, R) as r:
                for s in range(NS):
                    low(r, s + 1)
                    for c, stage in due(RANKS, s):
                        ranks(r, c, stage)
                    for c, _ in due(WEIGHTS, s):
                        weights(r, c)
                    if s % (FF // P) == FF // P - 1:
                        combine(r, *split_step(s)[:2])
            for c in range(NCH):
                v.wait_ge(last_ok, c + 1)
                xs = m.x[:, TPC * c:TPC * (c + 1), :]
                nc.vector.tensor_tensor(xs, xs, hid[(c + 3) % RING][:, :].rearrange("p (t e) -> p t e", e=E),
                                        ALU.add).then_inc(out_ok, 1)

        @block.gpsimd
        def _(pool):
            def parts(c, n):
                nc.gpsimd.tensor_copy(cur_hi[:, c, :], m.cur[:, c, :]).then_inc(hi_ok, 1)
                pool.wait_ge(hi_ok, n + 1)
                nc.gpsimd.tensor_tensor(cur_lo[:, c, :], m.cur[:, c, :], cur_hi[:, c, :],
                                        ALU.subtract).then_inc(cur_ok, 1)

            for c in range(NCH):
                parts(c, c)
            with pool.Fori(0, R) as r:
                for c in range(NCH):
                    for e in range(NE):
                        n = NE * (NCH * r + c) + e
                        pool.wait_ge(part_ok, n + 1 + PART_CREDIT)
                        pool.wait_ge(add_ok, n + ADD_CREDIT)
                        nc.gpsimd.tensor_tensor(m.cur[:, c, :], m.cur[:, c, :], part[:, e % 2, :],
                                                ALU.add).then_inc(add_ok, 1)
                    pool.wait_ge(hi_ok, NCH)
                    pool.wait_ge(add_ok, n + 1 + ADD_CREDIT)
                    parts(c, NCH * (r + 1) + c)

        @block.sync
        def _(sp):
            for c in range(NCH):
                sp.wait_ge(out_ok, c + 1)
                sp.dma_start(m.out.rearrange("b (t p) e -> p (b t) e", p=P)[:, TPC * c:TPC * (c + 1), :],
                             m.x[:, TPC * c:TPC * (c + 1), :]).then_inc(stored, 16)
            sp.wait_ge(stored, 16 * NCH)


def constants():
    def bf16_bits(a):
        return np.ascontiguousarray(a, np.float32).view(np.uint32) >> 16

    inv = 1.0 / 10000.0 ** (np.arange(0, D, 2, dtype=np.float32) / D)
    ang = np.outer(np.arange(T, dtype=np.float32), inv)
    pair = np.arange(P) % (HG * D) // HG // 2
    page = np.arange(T) // PAGE
    k_rows = np.zeros((P - ROW_ZERO, T), np.float32)
    k_rows[ROW_PAGE - ROW_ZERO:ROW_PAGE - ROW_ZERO + NPAGE] = page[None, :] == np.arange(NPAGE)[:, None]
    k_rows[ROW_MAX - ROW_ZERO:] = 1.0
    q_rows = np.zeros((ROW_MAX - ROW_ZERO, T), np.float32)
    q_rows[ROW_PAGE - ROW_ZERO:ROW_PAGE - ROW_ZERO + NPAGE] = np.where(page[None, :] < np.arange(NPAGE)[:, None], MASKED, 0.0)
    j, e = np.arange(NE)[None, :], np.arange(NE)[:, None]
    return {
        "cos": np.ascontiguousarray(np.cos(ang).T[pair]),
        "sin": np.ascontiguousarray(np.sin(ang).T[pair]),
        "ident": np.eye(P, dtype=np.float32),
        "k_rows": bf16_bits(k_rows).astype(np.uint16),
        "q_rows": bf16_bits(q_rows).astype(np.uint16),
        "tri": np.broadcast_to(np.stack([j < e, j > e]).astype(np.float32), (P, 2, NE, NE)).copy(),
    }


_INS = {
    "x": "L0_attn_x", "wq": "L0_attn_wq", "w_down": "L0_attn_w_down", "wk_up": "L0_attn_wk_up",
    "wv_up": "L0_attn_wv_up", "wo": "L0_attn_wo", "Wg": "L0_ffn_Wg", "bg": "L0_ffn_bg", "W1": "L0_ffn_W1",
    "b1": "L0_ffn_b1", "W2": "L0_ffn_W2", "b2": "L0_ffn_b2", "c": "L0_c", "wmod": "L0_wmod",
}


def kernel(**inputs):
    import concourse.bacc as bacc
    from concourse.bass_utils import run_bass_kernel_spmd

    nc = bacc.Bacc("TRN2", target_bir_lowering=False, num_devices=1)
    arrays, dram = {}, {}
    given = {name: np.ascontiguousarray(inputs[full]) for name, full in _INS.items()}
    for name in ("wq", "wk_up"):
        a = given[name]
        given[name] = np.ascontiguousarray(a.reshape(-1, NG, HG, D).transpose(0, 1, 3, 2).reshape(a.shape))
    given["c"] = np.ascontiguousarray(given["c"].T)
    given["Wg"] = np.ascontiguousarray(given["Wg"].transpose(1, 0, 2))
    given["bg"] = np.ascontiguousarray(np.broadcast_to(given["bg"][None, :, None, :], (P, R, 1, NE)))
    given["b1"] = np.ascontiguousarray(given["b1"].reshape(NE, FF // P, P).transpose(2, 0, 1))
    given["b2"] = np.ascontiguousarray(given["b2"].T)
    for name, a in {**given, **constants()}.items():
        arrays[f"in_{name}"] = a
        dram[name] = nc.dram_tensor(f"in_{name}", a.shape, mybir.dt.from_np(a.dtype), kind="ExternalInput").ap()
    out = nc.dram_tensor("out", (B, T, E), F32, kind="ExternalOutput").ap()
    adaln_block(nc, dram, out)
    return run_bass_kernel_spmd(nc, [arrays], core_ids=[0]).results[0]["out"]
```

```python
import concourse.bass as bass
import numpy as np
from concourse import mybir
from contextlib import ExitStack

F32 = mybir.dt.float32
F32R = mybir.dt.float32r
BF16 = mybir.dt.bfloat16
ALU = mybir.AluOpType
ACT = mybir.ActivationFunctionType
AX = mybir.AxisListType

P = 128
B, T, E = 2, 1024, 128
NH, D = 16, 8
LAT = 64
NE, R, FF = 4, 4, 512
PAGE = 32
TOK = B * T
NT = TOK // P
CH = 512
NCH = TOK // CH
TPC = CH // P
JB = T // P
HG = 4
NG = NH // HG
GROUPS = B * NG
SLOTS = 3
SCALE = float(D) ** -0.5
EPS = 1e-5

Q_PIECE = [0, 0, 0, 1, 1, 2]
K_PIECE = [0, 1, 2, 0, 1, 0]
TERMS = len(Q_PIECE)
ROW_ZERO = TERMS * D
ROW_PAGE = 64
ROW_MAX = P - 3
NPAGE = T // PAGE
MASKED = -3.0e38

UNITS = [
    [(0, 0, 0, 0, 512)],
    [(1, 0, 0, 0, 512)],
    [(0, 2, 0, 256, 256), (1, 6, 256, 256, 256)],
    [(0, 1, 0, 128, 384), (0, 3, 384, 384, 128)],
    [(1, 1, 0, 0, 512)],
    [(1, 2, 0, 0, 512)],
    [(1, 3, 0, 0, 512)],
    [(1, 4, 0, 0, 512)],
    [(1, 5, 0, 128, 384), (1, 7, 384, 384, 128)],
]
NU = len(UNITS)
FIRST_UNIT = [0, 1]
LAST_UNIT = [3, NU - 1]

BINS = [
    ([(0, 0), (4, 512)], 128, 0, 8),
    ([(1, 0), (5, 512)], 256, 1, 8),
    ([(2, 0)], 384, 2, 1),
    ([(6, 512)], 384, 10, 1),
    ([(3, 0)], 512, 3, 1),
    ([(4, 0)], 512, 4, 1),
    ([(5, 0)], 512, 5, 1),
    ([(6, 0)], 512, 6, 1),
    ([(7, 0)], 512, 7, 1),
    ([(7, 512)], 512, 11, 1),
]
GROUP_BINS = [(h, n) for h in range(HG) for n in range(len(BINS))]
NBINS = len(GROUP_BINS)
NB = NBINS + 1
LEAD = 4
CHAIN = 6
TURN_AFTER = 7
PARTS = [GROUP_BINS[u * NBINS // NU:(u + 1) * NBINS // NU] for u in range(NU)]
BEFORE = [u * NBINS // NU for u in range(NU)]


class Mem:

    def __init__(self, nc, stack):
        self.nc, self.stack = nc, stack

    def sb(self, name, shape, dt=F32):
        return self.stack.enter_context(self.nc.sbuf_tensor(name, shape, dt))

    def ps(self, name, shape, dt=F32):
        return self.stack.enter_context(self.nc.psum_tensor(name, shape, dt))

    def sem(self, name):
        return self.stack.enter_context(self.nc.semaphore(name))


def adaln_block(nc, w, out):
    with ExitStack() as stack:
        m = Mem(nc, stack)
        m.w, m.out = w, out
        m.qp = nc.dram_tensor("q_pieces", (3, GROUPS, HG * D, T), BF16).ap()
        m.kp = nc.dram_tensor("k_pieces", (3, GROUPS, HG * D, T), BF16).ap()
        m.x = m.sb("x_sb", [P, NT, E])
        m.ident = m.sb("ident", [P, P])
        m.identb = m.sb("identb", [P, P], BF16)
        m.modc = m.sb("modc", [P, 6, B])
        m.gbd = m.sb("gb_diag", [P, B, P])
        m.wog = m.sb("wog", [P, B, E])
        m.w1_hi = m.sb("w1_hi", [P, NE, FF], F32R)
        m.w1_lo = m.sb("w1_lo", [P, NE, FF], F32R)
        m.w2_hi = m.sb("w2_hi", [P, NE * FF // P, E], F32R)
        m.w2_lo = m.sb("w2_lo", [P, NE * FF // P, E], F32R)
        m.cur = m.sb("cur", [P, NCH, CH])
        m.mv = m.sb("mv", [P, NT, 2])
        m.stats = m.sb("stats", [P, NT, 6])
        m.ve = m.sb("ve", [P, NT, 1])
        m.sd = m.sb("sd", [P, NT, 1])
        m.rstd = m.sb("rstd", [P, NT, 1])
        m.nw = m.sb("nw", [P, NT, 1])
        m.wg = m.sb("wg_sb", [P, R + 1, NE])
        m.bg = m.sb("bg_sb", [P, R + 1, 1, NE])
        m.b1 = m.sb("b1_sb", [P, NE, FF // P])
        m.b2 = m.sb("b2_sb", [P, NE])
        m.tri = m.sb("tri", [P, 2, NE, NE])
        with ExitStack() as upto_attention:
            ma = Mem(nc, upto_attention)
            m.v = ma.sb("v_all", [P, GROUPS, JB, HG * D])
            m.ks = [ma.sb(f"ks{s}", [P, HG, T], BF16) for s in range(SLOTS)]
            m.qs = [ma.sb(f"qs{s}", [P, HG, T], BF16) for s in range(SLOTS)]
            m.qk_in = [ma.sem(f"qk_in{s}") for s in range(SLOTS)]
            with ExitStack() as part:
                prep(nc, m, Mem(nc, part))
            m.ovs = ma.sb("ovs", [P, GROUPS, 2, CH])
            with ExitStack() as part:
                attention(nc, m, Mem(nc, part))
            with ExitStack() as part:
                project(nc, m, Mem(nc, part))
        with ExitStack() as part:
            ffn(nc, m, Mem(nc, part))


def rstd_steps(nc, v, link, var_ok, sqrt_ok, m):
    nc.vector.tensor_scalar(m.ve[:, :, :], m.mv[:, :, 1:2], EPS, None, ALU.add).then_inc(var_ok, 1)
    v.wait_ge(sqrt_ok, 1)
    link(nc.vector.reciprocal(m.rstd[:, :, :], m.sd[:, :, :]))
    link(nc.vector.tensor_tensor(m.nw[:, :, :], m.rstd[:, :, :], m.rstd[:, :, :], ALU.mult))
    link(nc.vector.tensor_tensor(m.nw[:, :, :], m.nw[:, :, :], m.ve[:, :, :], ALU.mult))
    link(nc.vector.tensor_scalar(m.nw[:, :, :], m.nw[:, :, :], -0.5, 1.5, ALU.mult, ALU.add))
    link(nc.vector.tensor_tensor(m.rstd[:, :, :], m.rstd[:, :, :], m.nw[:, :, :], ALU.mult))


LOADS = [(0, 3), (3, 2), (5, 1)]


def load_group(sp, m, g, s):
    for first, n in LOADS:
        rows = slice(first * D, (first + n) * D)
        sp.dma_start(m.ks[s][rows, :, :],
                     m.kp[0:n, g].rearrange("c (d h) t -> c d (h t)", d=D)).then_inc(m.qk_in[s], 16)
        one = m.qp[Q_PIECE[first]:Q_PIECE[first] + 1, g].rearrange("c (d h) t -> c d (h t)", d=D)
        sp.dma_start(m.qs[s][rows, :, :], one.broadcast_to([n, D, HG * T])).then_inc(m.qk_in[s], 16)


def prep(nc, m, l):
    w = m.w
    ct, ce, sc = (l.sb(n, [P, B]) for n in ("ct", "ce", "sc"))
    wmod = l.sb("wmod", [P, 6 * E])
    wq, wqs = l.sb("wq", [E, E]), l.sb("wqs", [E, E])
    wd = l.sb("wd", [E, LAT])
    wk, wks = l.sb("wk", [LAT, E]), l.sb("wks", [LAT, E])
    wv = l.sb("wv", [LAT, E])
    wo = l.sb("wo", [E, E])
    cos, sin = l.sb("cos", [P, T]), l.sb("sin", [P, T])
    xn = l.sb("xn", [P, NT, E])
    lat = l.sb("lat", [LAT, 2, CH])
    ga = l.sb("ga", [P, B, E])
    gt, gs = l.sb("gt", [P, B, E]), l.sb("gs", [P, B, E])
    bt, bs = l.sb("bt", [P, B]), l.sb("bs", [P, B])
    rc = [l.sb(f"rc{s}", [P, CH]) for s in "qk"]
    rs = [l.sb(f"rs{s}", [P, CH]) for s in "qk"]
    ro = [l.sb(f"ro{s}", [P, 2, CH]) for s in "qk"]
    rr = [l.sb(f"rr{s}", [P, CH]) for s in "qk"]
    pieces = [l.sb(f"pieces_{s}", [P, NCH, 3, CH], BF16) for s in "qk"]
    turned = [l.ps(f"turned{i}", [P, CH]) for i in range(2)]
    pq = [l.ps(f"pq{i}", [P, CH]) for i in range(2)]
    pk = [l.ps(f"pk{i}", [P, CH]) for i in range(2)]
    plat = l.ps("plat", [P, CH])
    pmod = l.ps("pmod", [P, CH])

    in_c, in_mod, in_w, in_tab, in_rows = (l.sem(n) for n in ("in_c", "in_mod", "in_w", "in_tab", "in_rows"))
    in_x = [l.sem(f"in_x{c}") for c in range(NCH)]
    exp_c, silu_c, mods, mod_read = (l.sem(n) for n in ("exp_c", "silu_c", "mods", "mod_read"))
    var_ok, sqrt_ok, xn_ok, turn_ok, h_ok = (l.sem(n) for n in ("var_ok", "sqrt_ok", "xn_ok", "turn_ok", "h_ok"))
    swap_ok, q_ok, lat_ok, lat_sb, k_ok, v_ok, v_sb = (
        l.sem(n) for n in ("swap_ok", "q_ok", "lat_ok", "lat_sb", "k_ok", "v_ok", "v_sb"))
    rot, rot_read = l.sem("rot"), l.sem("rot_read")
    piece0, piece1, piece2, rest = (l.sem(n) for n in ("piece0", "piece1", "piece2", "rest"))
    dve, zeroed, pieces_out = l.sem("dve_prep"), l.sem("zeroed"), l.sem("pieces_out")

    with nc.Block() as block:

        @block.sync
        def _(sp):
            x_dram = w["x"].rearrange("b (t p) e -> p (b t) e", p=P)
            for c in range(NCH):
                sp.dma_start(m.x[:, TPC * c:TPC * (c + 1), :], x_dram[:, TPC * c:TPC * (c + 1), :]).then_inc(in_x[c], 16)
            for s in range(SLOTS):
                for rows, dst in ((w["k_rows"].bitcast(BF16), m.ks[s]), (w["q_rows"].bitcast(BF16), m.qs[s])):
                    n = rows.shape[0]
                    sp.dma_start(dst[ROW_ZERO:ROW_ZERO + n, :, :],
                                 rows.rearrange("r (h t) -> r h t", h=1).broadcast_to([n, HG, T])).then_inc(in_rows, 16)
            for c in range(NCH):
                b, at = c // 2, slice(CH * (c % 2), CH * (c % 2) + CH)
                for side, dst in enumerate((m.qp, m.kp)):
                    n = 2 * c + side + 1
                    sp.wait_ge(piece0, n)
                    sp.wait_ge(piece1, n)
                    sp.wait_ge(piece2, n)
                    sp.dma_start(dst.rearrange("c g r t -> (g r) c t")[b * P:(b + 1) * P, :, at],
                                 pieces[side][:, c, :, :]).then_inc(pieces_out, 16)
                if c == 1:
                    sp.wait_ge(pieces_out, 16 * 4)
                    load_group(sp, m, 0, 0)
                    load_group(sp, m, 1, 1)
            sp.wait_ge(in_rows, 16 * SLOTS * 2)
            sp.wait_ge(pieces_out, 16 * NCH * 2)

        @block.scalar
        def _(act):
            act.dma_start(ct[:, :], w["c"]).then_inc(in_c, 16)
            act.dma_start(wmod[:, :], w["wmod"]).then_inc(in_mod, 16)
            act.dma_start(m.ident[:, :], w["ident"]).then_inc(in_mod, 16)
            for dst, name in ((wq, "wq"), (wd, "w_down"), (wk, "wk_up"), (wv, "wv_up"), (wo, "wo")):
                act.dma_start(dst[:, :], w[name]).then_inc(in_w, 16)
            act.dma_start(cos[:, :], w["cos"]).then_inc(in_tab, 16)
            act.dma_start(sin[:, :], w["sin"]).then_inc(in_tab, 16)
            act.wait_ge(in_c, 16)
            nc.scalar.activation(ce[:, :], ct[:, :], ACT.Exp, scale=-1.0).then_inc(exp_c, 1)
            act.wait_ge(var_ok, 1)
            nc.scalar.activation(m.sd[:, :, :], m.ve[:, :, :], ACT.Sqrt).then_inc(sqrt_ok, 1)

            def hidden(c):
                b = c // 2
                act.wait_ge(turn_ok, c + 1)
                nc.scalar.activation(m.cur[:, c, :], turned[c % 2][:, :], ACT.Identity,
                                     bias=m.modc[:, 0, b:b + 1], scale=m.modc[:, 1, b:b + 1]).then_inc(h_ok, 1)

            def first_piece(c, side):
                act.wait_ge(rot, 2 * c + side + 1)
                nc.scalar.activation(pieces[side][:, c, 0, :], ro[side][:, c % 2, :], ACT.Copy).then_inc(piece0, 1)

            def second_piece(c, side):
                act.wait_ge(rest, 2 * c + side + 1)
                nc.scalar.activation(pieces[side][:, c, 1, :], rr[side][:, :], ACT.Copy).then_inc(piece1, 1)

            act.wait_ge(mod_read, 1)
            hidden(0)
            for c in range(NCH + 1):
                if c < NCH:
                    act.wait_ge(lat_ok, c + 1)
                    nc.scalar.activation(lat[:, c % 2, :], plat[0:LAT, :], ACT.Copy).then_inc(lat_sb, 1)
                if c + 1 < NCH:
                    hidden(c + 1)
                if c >= 1:
                    first_piece(c - 1, 0)
                    first_piece(c - 1, 1)
                    second_piece(c - 1, 0)
                    second_piece(c - 1, 1)
                if c < NCH:
                    b, j = c // 2, TPC * (c % 2)
                    act.wait_ge(v_ok, c + 1)
                    nc.scalar.activation(m.v[:, b * NG:(b + 1) * NG, j:j + TPC, :],
                                         pmod[:, :].rearrange("p (j g r) -> p g j r", j=TPC, g=NG),
                                         ACT.Copy).then_inc(v_sb, 1)

        @block.gpsimd
        def _(pool):
            for c in range(NCH):
                for side in range(2):
                    n = 2 * c + side
                    pool.wait_ge(piece0, n + 1)
                    if n >= 2:
                        pool.wait_ge(piece1, n - 1)
                        pool.wait_ge(piece2, n - 1)
                    nc.gpsimd.tensor_tensor(rr[side][:, :], ro[side][:, c % 2, :], pieces[side][:, c, 0, :],
                                            ALU.subtract).then_inc(rest, 1)
                for side in range(2):
                    n = 2 * c + side
                    pool.wait_ge(piece1, n + 1)
                    pool.wait_ge(rest, n + 1)
                    nc.gpsimd.tensor_tensor(pieces[side][:, c, 2, :], rr[side][:, :], pieces[side][:, c, 1, :],
                                            ALU.subtract).then_inc(piece2, 1)

        @block.vector
        def _(v):
            links = [0]

            def link(ins):
                links[0] += 1
                ins.then_inc(dve, 1)
                v.wait_ge(dve, links[0])

            for c in range(NCH):
                v.wait_ge(in_x[c], 16)
                for t in range(TPC * c, TPC * c + TPC):
                    s = nc.vector.bn_stats(m.stats[:, t, :], m.x[:, t, :])
                if c == 1:
                    v.wait_ge(exp_c, 1)
                    link(nc.vector.tensor_scalar(ce[:, :], ce[:, :], 1.0, None, ALU.add))
                    link(nc.vector.reciprocal(ce[:, :], ce[:, :]))
                    nc.vector.tensor_tensor(sc[:, :], ct[:, :], ce[:, :], ALU.mult).then_inc(silu_c, 1)
            link(s)
            for t in range(NT):
                s = nc.vector.bn_aggr(m.mv[:, t, :], m.stats[:, t, :])
            link(s)

            rstd_steps(nc, v, link, var_ok, sqrt_ok, m)
            v.wait_ge(mods, 1)
            link(nc.vector.tensor_copy(m.modc[:, :, :], pmod[:, 0:6 * B].rearrange("p (i b) -> p i b", b=B)))
            for i in (1, 4):
                s = nc.vector.tensor_scalar(m.modc[:, i, :], m.modc[:, i, :], 1.0, None, ALU.add)
            s.then_inc(mod_read, 1)
            for c in range(NCH):
                for t in range(TPC * c, TPC * c + TPC):
                    s = nc.vector.tensor_scalar(xn[:, t, :], m.x[:, t, :], m.mv[:, t, 0:1], m.rstd[:, t, :],
                                                ALU.subtract, ALU.mult)
                s.then_inc(xn_ok, 1)
                if c == 0:
                    v.wait_ge(in_w, 80)
                    for dst, src in ((wqs, wq), (wks, wk)):
                        pd, ps = (a[:, :].rearrange("p (i two h) -> p i two h", two=2, h=HG) for a in (dst, src))
                        nc.vector.tensor_scalar(pd[:, :, 0:1, :], ps[:, :, 1:2, :], -1.0, None, ALU.mult)
                        s = nc.vector.tensor_copy(pd[:, :, 1:2, :], ps[:, :, 0:1, :])
                    s.then_inc(swap_ok, 1)
                    nc.vector.tensor_copy(m.identb[:, :], m.ident[:, :])
                    nc.vector.tensor_copy(ga[:, :, :], pmod[:, E:E + B * E].rearrange("p (b e) -> p b e", b=B))\
                        .then_inc(mod_read, 1)
            v.wait_ge(in_tab, 32)
            for c in range(NCH):
                tab = slice(CH * (c % 2), CH * (c % 2) + CH)
                for side, (ready, pp) in enumerate(((q_ok, pq), (k_ok, pk))):
                    n = 2 * c + side
                    v.wait_ge(ready, c + 1)
                    nc.vector.tensor_tensor(rc[side][:, :], pp[0][:, :], cos[:, tab], ALU.mult)
                    s = nc.vector.tensor_tensor(rs[side][:, :], pp[1][:, :], sin[:, tab], ALU.mult)
                    s.then_inc(rot_read, 1)
                    v.wait_ge(rot_read, n + 1)
                    if c >= 2:
                        v.wait_ge(piece0, n - 3)
                        v.wait_ge(rest, n - 3)
                    nc.vector.tensor_tensor(ro[side][:, c % 2, :], rc[side][:, :], rs[side][:, :], ALU.add).then_inc(rot, 1)
            for g, t, s in ((ga[:, :, :], gt[:, :, :], gs[:, :, :]), (m.modc[:, 5, :], bt[:, :], bs[:, :])):
                link(nc.vector.tensor_scalar(t, g, -1.0, None, ALU.mult))
                link(nc.vector.tensor_tensor(t, t, g, ALU.max))
                link(nc.vector.tensor_scalar(t, t, 0.25, None, ALU.max))
                link(nc.vector.tensor_scalar(s, g, 0.0, 2.0, ALU.is_ge, ALU.mult))
                link(nc.vector.tensor_scalar(s, s, -1.0, None, ALU.add))
                link(nc.vector.tensor_tensor(t, t, s, ALU.mult))
            for b in range(B):
                nc.vector.tensor_tensor(m.wog[:, b, :], wo[:, :], gt[:, b, :], ALU.mult)
                nc.vector.tensor_scalar(m.gbd[:, b, :], m.ident[:, :], bt[:, b:b + 1], None, ALU.mult)

        @block.tensor
        def _(pe):
            pe.wait_ge(silu_c, 1)
            pe.wait_ge(in_mod, 32)
            for i in range(6):
                nc.tensor.matmul(pmod[:, i * B:(i + 1) * B], wmod[:, i * E:(i + 1) * E], sc[:, :], start=True, stop=True)
            for b in range(B):
                mm = nc.tensor.matmul(pmod[:, E + b * E:E + (b + 1) * E], sc[:, b:b + 1].broadcast_to([P, P]),
                                      wmod[:, 2 * E:3 * E], start=True, stop=True)
            mm.then_inc(mods, 1)

            def turn(c):
                pe.wait_ge(xn_ok, c + 1)
                if c >= 2:
                    pe.wait_ge(h_ok, c - 1)
                for i in range(TPC):
                    mm = nc.tensor.transpose(turned[c % 2][:, i * P:(i + 1) * P], xn[:, TPC * c + i, :], m.ident[:, :])
                mm.then_inc(turn_ok, 1)

            turn(0)
            pe.wait_ge(swap_ok, 1)
            for c in range(NCH):
                pe.wait_ge(h_ok, c + 1)
                if c >= 1:
                    pe.wait_ge(lat_sb, c)
                nc.tensor.matmul(plat[0:LAT, :], wd[:, :], m.cur[:, c, :], start=True, stop=True).then_inc(lat_ok, 1)
                if c + 1 < NCH:
                    turn(c + 1)
                if c >= 1:
                    pe.wait_ge(rot_read, 2 * c)
                nc.tensor.matmul(pq[0][:, :], wq[:, :], m.cur[:, c, :], start=True, stop=True)
                nc.tensor.matmul(pq[1][:, :], wqs[:, :], m.cur[:, c, :], start=True, stop=True).then_inc(q_ok, 1)
                pe.wait_ge(lat_sb, c + 1)
                nc.tensor.matmul(pk[0][:, :], wk[:, :], lat[:, c % 2, :], start=True, stop=True)
                nc.tensor.matmul(pk[1][:, :], wks[:, :], lat[:, c % 2, :], start=True, stop=True).then_inc(k_ok, 1)
                if c == 0:
                    pe.wait_ge(mod_read, 2)
                if c >= 1:
                    pe.wait_ge(v_sb, c)
                for i in range(TPC):
                    mm = nc.tensor.matmul(pmod[:, i * P:(i + 1) * P], lat[:, c % 2, i * P:(i + 1) * P], wv[:, :],
                                          start=True, stop=True)
                mm.then_inc(v_ok, 1)


def attention(nc, m, l):
    ST_RING, MX_RING = 3, 3
    probs = [l.sb(f"probs{s}", [P, HG, CH]) for s in range(SLOTS)]
    vs = [l.sb(f"vs{s}", [P, JB, HG, 32]) for s in range(SLOTS)]
    mcol = [l.sb(f"mcol{s}", [P, HG, 12]) for s in range(SLOTS)]
    mres = l.sb("mres", [P, HG, JB])
    mpc = l.sb("mpc", [P, 3, HG, JB], BF16)
    mrow = l.sb("mrow", [3 * HG * JB, P], BF16)
    w1_raw = l.sb("w1_raw", [P, NE, FF])
    w2_raw = l.sb("w2_raw", [P, NE * FF // P, E])
    st = l.ps("st", [P, ST_RING, CH])
    ov = l.ps("ov", [P, 2, CH])
    mx = l.ps("mx", [P, MX_RING, CH])

    mrow_in = [l.sem(f"mrow_in{s}") for s in range(SLOTS)]
    st_done, exp_done, pv_done, ov_read = (l.sem(n) for n in ("st_done", "exp_done", "pv_done", "ov_read"))
    bin_full, bin_read, mchain = (l.sem(n) for n in ("bin_full", "bin_read", "mchain"))
    vs_init, vs_ok, w_in, w_hi, w_lo, small_in = (
        l.sem(n) for n in ("vs_init", "vs_ok", "w_in", "w_hi", "w_lo", "small_in"))
    ST_CREDIT, EXP_CREDIT, PV_CREDIT, OV_CREDIT = 1, ST_RING, SLOTS, 2

    def gnum(i, a):
        return SLOTS * i + a

    def exists(i, a):
        return not isinstance(i, int) or SLOTS * i + a < GROUPS

    def uses(i, a):
        return i + (a // SLOTS + 1)

    def place(i, a, k):
        if isinstance(i, int) and gnum(i, a) == 0:
            return k + 1
        return k if k <= TURN_AFTER else k + 1

    def turn_place(i, a):
        return 0 if isinstance(i, int) and gnum(i, a) == GROUPS - 1 else TURN_AFTER + 1

    def in_stream(i, a, at):
        return NB * gnum(i, a) + (at - 1)

    def all_groups(eng, body):
        whole = (GROUPS - 2) // SLOTS
        with eng.Fori(0, whole) as i:
            for a in range(SLOTS):
                body(i, a)
        for g in range(whole * SLOTS, GROUPS):
            body(whole, g - whole * SLOTS)

    def following(i, a, u):
        return (i, a, u + 1) if u + 1 < NU else (i, a + 1, 0)

    def part_at(i, a, u):
        n = u + LEAD
        return (i, a + 1, n) if n < NU else (i, a + 2, n - NU)

    with nc.Block() as block:

        @block.sync
        def _(sp):
            def max_rows(i, a):
                s = a % SLOTS
                sp.wait_ge(bin_read, in_stream(i, a + 1, turn_place(i, a)) + 1)
                sp.dma_start(m.qs[s][ROW_MAX:ROW_MAX + 3, :, :], mrow[:, :]).then_inc(mrow_in[s], 16)

            def body(i, a):
                if exists(i, a + 2):
                    sp.wait_ge(st_done, HG * NU * gnum(i, a) + ST_CREDIT)
                    load_group(sp, m, gnum(i, a + 2), (a + 2) % SLOTS)
                if exists(i, a + 1):
                    max_rows(i, a + 1)

            max_rows(0, 0)
            sp.dma_start(w1_raw[:, :, :], m.w["W1"].rearrange("e h f -> h e f")).then_inc(w_in, 16)
            sp.dma_start(w2_raw[:, :, :], m.w["W2"].rearrange("e (c f) h -> f (e c) h", f=P)).then_inc(w_in, 16)
            sp.dma_start(m.wg[:, 0:R, :], m.w["Wg"]).then_inc(small_in, 16)
            sp.dma_start(m.wg[:, R:R + 1, :], m.w["Wg"][:, R - 1:R, :]).then_inc(small_in, 16)
            sp.dma_start(m.bg[:, 0:R, :, :], m.w["bg"]).then_inc(small_in, 16)
            sp.dma_start(m.bg[:, R:R + 1, :, :], m.w["bg"][:, R - 1:R, :, :]).then_inc(small_in, 16)
            sp.dma_start(m.b1[:, :, :], m.w["b1"]).then_inc(small_in, 16)
            sp.dma_start(m.b2[:, :], m.w["b2"]).then_inc(small_in, 16)
            sp.dma_start(m.tri[:, :, :, :], m.w["tri"]).then_inc(small_in, 16)
            all_groups(sp, body)
            sp.wait_ge(small_in, 112)

        @block.gpsimd
        def _(pool):
            def stage(i, a):
                s = a % SLOTS
                nc.gpsimd.tensor_copy(vs[s][:, :, :, 0:D],
                                      m.v[:, gnum(i, a), :, :].rearrange("p j (h d) -> p j h d", d=D)).then_inc(vs_ok, 1)

            for s in range(SLOTS):
                nc.gpsimd.memset(vs[s][:, :, :, :], 0.0).then_inc(vs_init, 1)
            pool.wait_ge(vs_init, SLOTS)
            for s in range(SLOTS):
                nc.gpsimd.memset(vs[s][:, :, :, D:D + 1], 1.0).then_inc(vs_init, 1)
            pool.wait_ge(vs_init, 2 * SLOTS)
            stage(0, 0)
            stage(0, 1)
            pool.wait_ge(w_in, 32)
            for e in range(NE):
                c = slice(e * FF // P, (e + 1) * FF // P)
                nc.gpsimd.tensor_copy(m.w1_hi[:, e, :], w1_raw[:, e, :])
                nc.gpsimd.tensor_copy(m.w2_hi[:, c, :], w2_raw[:, c, :]).then_inc(w_hi, 1)
                pool.wait_ge(w_hi, e + 1)
                nc.gpsimd.tensor_tensor(m.w1_lo[:, e, :], w1_raw[:, e, :], m.w1_hi[:, e, :], ALU.subtract)
                nc.gpsimd.tensor_tensor(m.w2_lo[:, c, :], w2_raw[:, c, :], m.w2_hi[:, c, :],
                                        ALU.subtract).then_inc(w_lo, 1)

            def body(i, a):
                if exists(i, a + 2):
                    pool.wait_ge(vs_init, 2 * SLOTS)
                    pool.wait_ge(pv_done, NU * gnum(i, a) + PV_CREDIT)
                    stage(i, a + 2)

            all_groups(pool, body)

        @block.scalar
        def _(act):
            def exps(i, a, u):
                n = NU * gnum(i, a) + u
                for h in range(HG):
                    act.wait_ge(st_done, HG * n + h + 1 + ST_CREDIT)
                    if h == 0:
                        act.wait_ge(pv_done, n + 1 - SLOTS + PV_CREDIT)
                    nc.scalar.activation(probs[u % SLOTS][:, h, :], st[:, (HG * u + h) % ST_RING, :], ACT.Exp,
                                         scale=SCALE).then_inc(exp_done, 1)

            def keep_output(i, a, c):
                g = gnum(i, a)
                act.wait_ge(pv_done, NU * g + LAST_UNIT[c] + 1 + PV_CREDIT)
                nc.scalar.activation(m.ovs[:, g, c, :], ov[:, c, :], ACT.Copy).then_inc(ov_read, 1)

            def body(i, a):
                for u in range(NU):
                    if exists(*following(i, a, u)[:2]):
                        exps(*following(i, a, u))
                    if u == LAST_UNIT[0] + 1:
                        keep_output(i, a, 0)
                keep_output(i, a, 1)

            exps(0, 0, 0)
            all_groups(act, body)

        @block.vector
        def _(v):
            def read_bin(i, a, k):
                h, b = GROUP_BINS[k]
                blocks, keys, slot, step = BINS[b]
                at = place(i, a, k)
                v.wait_ge(bin_full, in_stream(i, a, at) + 1)
                nc.vector.tensor_reduce(mcol[a % SLOTS][:, h, slot:slot + step * (len(blocks) - 1) + 1:step],
                                        mx[:, at % MX_RING, 0:len(blocks) * keys].rearrange("p (b k) -> p b k", k=keys),
                                        AX.X, ALU.max, negate=True).then_inc(bin_read, 1)

            def take_apart(i, a, x):
                if x == 0:
                    v.wait_ge(bin_read, in_stream(i, a, NB))
                else:
                    v.wait_ge(mchain, CHAIN * gnum(i, a) + x)
                mc = mcol[a % SLOTS]
                nm, res = mc[:, :, 0:JB], mres[:, :, :]
                piece = [mpc[:, n, :, :] for n in range(3)]
                if x == 0:
                    step = nc.vector.tensor_tensor(mc[:, :, 4:8], mc[:, :, 4:8], mc[:, :, 8:12], ALU.min)
                elif x == 1:
                    step = nc.vector.tensor_copy(piece[0], nm)
                elif x == 2:
                    step = nc.vector.tensor_tensor(res, nm, piece[0], ALU.subtract)
                elif x == 3:
                    step = nc.vector.tensor_copy(piece[1], res)
                elif x == 4:
                    step = nc.vector.tensor_tensor(res, res, piece[1], ALU.subtract)
                else:
                    step = nc.vector.tensor_copy(piece[2], res)
                step.then_inc(mchain, 1)

            def keep_rows(i, a):
                at = turn_place(i, a)
                v.wait_ge(bin_full, in_stream(i, a + 1, at) + 1)
                if not isinstance(i, int) or gnum(i, a) > 0:
                    v.wait_ge(mrow_in[(a - 1) % SLOTS], 16 * uses(i, a - 1))
                nc.vector.tensor_copy(mrow[:, :], mx[0:3 * HG * JB, at % MX_RING, 0:P // 2].bitcast(BF16))\
                    .then_inc(bin_read, 1)

            def part(i, a, p):
                first = isinstance(i, int) and gnum(i, a) == 0
                if p == 0 and not first:
                    take_apart(i, a - 1, 0)
                for k in range(BEFORE[p], BEFORE[p] + len(PARTS[p])):
                    read_bin(i, a, k)
                    if k + 1 < CHAIN and not first:
                        take_apart(i, a - 1, k + 1)
                    if k == TURN_AFTER and not first:
                        keep_rows(i, a - 1)

            def body(i, a):
                for u in range(NU):
                    ni, na, p = part_at(i, a, u)
                    if exists(ni, na):
                        part(ni, na, p)
                    elif p == 0 and exists(i, a + 1):
                        for x in range(CHAIN):
                            take_apart(i, a + 1, x)
                        keep_rows(i, a + 1)

            for p in range(NU):
                part(0, 0, p)
            for p in range(LEAD):
                part(0, 1, p)
            all_groups(v, body)

        @block.tensor
        def _(pe):
            def scores(i, a, u, h):
                s, n = a % SLOTS, HG * (NU * gnum(i, a) + u) + h
                if u == 0 and h == 0:
                    pe.wait_ge(m.qk_in[s], 16 * 2 * len(LOADS) * uses(i, a))
                    pe.wait_ge(mrow_in[s], 16 * uses(i, a))
                pe.wait_ge(exp_done, n + 1 - ST_RING + EXP_CREDIT)
                for c, j, off, q0, nq in UNITS[u]:
                    mm = nc.tensor.matmul(st[:, (HG * u + h) % ST_RING, off:off + nq],
                                          m.ks[s][:, h, j * P:(j + 1) * P],
                                          m.qs[s][:, h, c * CH + q0:c * CH + q0 + nq], start=True, stop=True)
                mm.then_inc(st_done, 1)

            def weigh(i, a, u, half):
                s, g = a % SLOTS, gnum(i, a)
                if half == 0:
                    pe.wait_ge(exp_done, HG * (NU * g + u + 1) + EXP_CREDIT)
                    if u == FIRST_UNIT[0]:
                        pe.wait_ge(vs_ok, g + 1)
                    for c in range(2):
                        if u == FIRST_UNIT[c]:
                            pe.wait_ge(ov_read, 2 * g - 1 + c + OV_CREDIT)
                for c, j, off, q0, nq in UNITS[u]:
                    lo, hi = max(off, half * CH // 2), min(off + nq, (half + 1) * CH // 2)
                    if lo >= hi:
                        continue
                    for h in range(HG):
                        mm = nc.tensor.matmul(ov[32 * h:32 * h + 32, c, q0 + lo - off:q0 + hi - off],
                                              vs[s][:, j, h, :], probs[u % SLOTS][:, h, lo:hi],
                                              start=(u == FIRST_UNIT[c] and half == 0),
                                              stop=(u == LAST_UNIT[c] and half == 1),
                                              skip_group_check=True)
                if half == 1:
                    mm.then_inc(pv_done, 1)

            def free_bank(i, a, at):
                n = in_stream(i, a, at)
                if not isinstance(n, int) or n >= MX_RING:
                    pe.wait_ge(bin_read, n - 1 if at < 2 else n + 1 - MX_RING)

            def fill_bin(i, a, k):
                s, at = a % SLOTS, place(i, a, k)
                h, b = GROUP_BINS[k]
                if k == 0:
                    pe.wait_ge(m.qk_in[s], 16 * 2 * len(LOADS) * uses(i, a))
                free_bank(i, a, at)
                blocks, keys, _, _ = BINS[b]
                for x, (t, k0) in enumerate(blocks):
                    mm = nc.tensor.matmul(mx[:, at % MX_RING, x * keys:(x + 1) * keys],
                                          m.qs[s][0:ROW_MAX, h, t * P:(t + 1) * P],
                                          m.ks[s][0:ROW_MAX, h, k0:k0 + keys], start=True, stop=True)
                mm.then_inc(bin_full, 1)

            def turn_maxima(i, a):
                at = turn_place(i, a)
                pe.wait_ge(mchain, CHAIN * (gnum(i, a) + 1))
                free_bank(i, a + 1, at)
                nc.tensor.transpose(mx[0:3 * HG * JB, at % MX_RING, 0:P // 2].bitcast(BF16),
                                    mpc[:, :, :, :].rearrange("p c h t -> p (c h t)"),
                                    m.identb[:, :]).then_inc(bin_full, 1)

            def part(i, a, p, quarter):
                n = len(PARTS[p])
                for k in range(BEFORE[p] + n * quarter // 4, BEFORE[p] + n * (quarter + 1) // 4):
                    fill_bin(i, a, k)
                    if k == TURN_AFTER and not (isinstance(i, int) and gnum(i, a) == 0):
                        turn_maxima(i, a - 1)

            def body(i, a):
                for u in range(NU):
                    nxt, side = following(i, a, u), part_at(i, a, u)
                    for half in range(2):
                        if exists(*nxt[:2]):
                            scores(*nxt, 2 * half)
                            scores(*nxt, 2 * half + 1)
                        if exists(*side[:2]):
                            part(*side, 2 * half)
                        weigh(i, a, u, half)
                        if exists(*side[:2]):
                            part(*side, 2 * half + 1)
                    if side[2] == 0 and exists(i, a + 1) and not exists(*side[:2]):
                        turn_maxima(i, a + 1)

            nc.tensor.sem_inc(st_done, ST_CREDIT)
            nc.tensor.sem_inc(exp_done, EXP_CREDIT)
            nc.tensor.sem_inc(pv_done, PV_CREDIT)
            nc.tensor.sem_inc(ov_read, OV_CREDIT)
            for a, parts in ((0, NU), (1, LEAD)):
                for p in range(parts):
                    for quarter in range(4):
                        part(0, a, p, quarter)
            for h in range(HG):
                scores(0, 0, 0, h)
            all_groups(pe, body)


def project(nc, m, l):
    rec = l.sb("rec", [P, 2, NH, 1])
    att = l.sb("att", [P, 2, NH, D])
    att_t = l.sb("att_t", [P, 2, P])
    xn = l.sb("xn2", [P, NT, E])
    heads = [l.ps(f"heads{i}", [P, CH]) for i in range(2)]
    turn = [l.ps(f"turn{i}", [P, CH]) for i in range(2)]
    added = [l.ps(f"added{i}", [P, CH]) for i in range(2)]
    h_t = [l.ps(f"h_t{i}", [P, CH]) for i in range(2)]
    heads_ok, rec_ok, att_ok, turn_ok, att_sb, add_ok, x_ok = (
        l.sem(n) for n in ("heads_ok", "rec_ok", "att_ok", "turn2_ok", "att_sb", "add_ok", "x_ok"))
    dve, var_ok, sqrt_ok, xn_ok, ht_ok, h_ok = (
        l.sem(n) for n in ("dve_proj", "var2_ok", "sqrt2_ok", "xn2_ok", "ht_ok", "h2_ok"))

    with nc.Block() as block:

        @block.tensor
        def _(pe):
            def to_tokens(t):
                if t >= 2:
                    pe.wait_ge(att_ok, t - 1)
                b, c, i = t // JB, t % JB // TPC, t % TPC
                for hg in range(NG):
                    mm = nc.tensor.transpose(heads[t % 2][:, hg * P:(hg + 1) * P],
                                             m.ovs[:, b * NG + hg, c, i * P:(i + 1) * P], m.ident[:, :])
                mm.then_inc(heads_ok, 1)

            def back(t):
                pe.wait_ge(att_ok, t + 1)
                if t >= 2:
                    pe.wait_ge(att_sb, t - 1)
                nc.tensor.transpose(turn[t % 2][:, 0:P], att[:, t % 2, :, :].rearrange("p h d -> p (h d)"),
                                    m.ident[:, :]).then_inc(turn_ok, 1)

            def wo(t):
                pe.wait_ge(att_sb, t + 1)
                if t >= 2:
                    pe.wait_ge(x_ok, t - 1)
                nc.tensor.matmul(added[t % 2][:, 0:E], att_t[:, t % 2, :], m.wog[:, t // JB, :],
                                 start=True, stop=True).then_inc(add_ok, 1)

            for t in range(NT + 2):
                if t < NT:
                    to_tokens(t)
                if 1 <= t <= NT:
                    back(t - 1)
                if t >= 2:
                    wo(t - 2)
            for c in range(NCH):
                pe.wait_ge(xn_ok, c + 1)
                if c >= 2:
                    pe.wait_ge(h_ok, c - 1)
                for i in range(TPC):
                    mm = nc.tensor.transpose(h_t[c % 2][:, i * P:(i + 1) * P], xn[:, TPC * c + i, :], m.ident[:, :])
                mm.then_inc(ht_ok, 1)

        @block.scalar
        def _(act):
            for t in range(NT):
                act.wait_ge(turn_ok, t + 1)
                if t >= 2:
                    act.wait_ge(add_ok, t - 1)
                nc.scalar.activation(att_t[:, t % 2, :], turn[t % 2][:, 0:P], ACT.Copy).then_inc(att_sb, 1)
            act.wait_ge(var_ok, 1)
            nc.scalar.activation(m.sd[:, :, :], m.ve[:, :, :], ACT.Sqrt).then_inc(sqrt_ok, 1)
            for c in range(NCH):
                b = c // 2
                act.wait_ge(ht_ok, c + 1)
                nc.scalar.activation(m.cur[:, c, :], h_t[c % 2][:, :], ACT.Identity,
                                     bias=m.modc[:, 3, b:b + 1], scale=m.modc[:, 4, b:b + 1]).then_inc(h_ok, 1)

        @block.vector
        def _(v):
            links = [0]

            def link(ins):
                links[0] += 1
                ins.then_inc(dve, 1)
                v.wait_ge(dve, links[0])

            def divide(t):
                v.wait_ge(heads_ok, t + 1)
                if t >= 2:
                    v.wait_ge(turn_ok, t - 1)
                o = heads[t % 2][:, :].rearrange("p (h r) -> p h r", r=32)
                nc.vector.reciprocal(rec[:, t % 2, :, :], o[:, :, D:D + 1]).then_inc(rec_ok, 1)
                v.wait_ge(rec_ok, t + 1)
                nc.vector.tensor_tensor(att[:, t % 2, :, :], o[:, :, 0:D],
                                        rec[:, t % 2, :, :].broadcast_to([P, NH, D]), ALU.mult).then_inc(att_ok, 1)

            def residual(t):
                v.wait_ge(add_ok, t + 1)
                nc.vector.tensor_tensor(m.x[:, t, :], m.x[:, t, :], added[t % 2][:, 0:E], ALU.add).then_inc(x_ok, 1)
                v.wait_ge(x_ok, t + 1)
                return nc.vector.bn_stats(m.stats[:, t, :], m.x[:, t, :])

            for t in range(NT + 2):
                if t < NT:
                    divide(t)
                if t >= 2:
                    last = residual(t - 2)
            link(last)
            for t in range(NT):
                last = nc.vector.bn_aggr(m.mv[:, t, :], m.stats[:, t, :])
            link(last)
            rstd_steps(nc, v, link, var_ok, sqrt_ok, m)
            for c in range(NCH):
                for t in range(TPC * c, TPC * c + TPC):
                    last = nc.vector.tensor_scalar(xn[:, t, :], m.x[:, t, :], m.mv[:, t, 0:1], m.rstd[:, t, :],
                                                   ALU.subtract, ALU.mult)
                last.then_inc(xn_ok, 1)


def ffn(nc, m, l):
    K = NE * FF // P
    NS = NCH * K
    AHEAD, RING = 3, 4
    cur_hi = l.sb("cur_hi", [P, NCH, CH], F32R)
    cur_lo = l.sb("cur_lo", [P, NCH, CH], F32R)
    gel = [l.sb(f"gel{i}", [P, CH]) for i in range(RING)]
    gel_hi = [l.sb(f"gel_hi{i}", [P, CH], F32R) for i in range(RING)]
    gel_lo = [l.sb(f"gel_lo{i}", [P, CH], F32R) for i in range(RING)]
    cwb = l.sb("cwb", [P, NE, CH])
    part = l.sb("part", [P, 2, CH])
    log = l.sb("log", [P, TPC, NE])
    ge, gt = l.sb("at_least", [P, TPC, NE, NE]), l.sb("above", [P, TPC, NE, NE])
    rank, half, hdiff, dl = (l.sb(n, [P, TPC, NE]) for n in ("rank", "half", "hdiff", "dl"))
    gap, th = l.sb("gap", [P, TPC, 1]), l.sb("th", [P, TPC, 1])
    cw = l.sb("cw", [P, TPC, NE])
    hid = [l.ps(f"hid{i}", [P, CH]) for i in range(RING)]
    y = [l.ps(f"y{i}", [P, CH]) for i in range(2)]
    plog = l.ps("plog", [P, CH])
    pcw = l.ps("pcw", [P, CH])

    cur_ok, hi_ok, hid_ok, gel_ok, lo_ok, y_ok = (
        l.sem(n) for n in ("cur_ok", "hi_ok", "hid_ok", "gel_ok", "lo_ok", "y_ok"))
    log_ok, gap_ok, th_ok, cw_ok, pcw_ok, cwb_ok, part_ok, add_ok, chain = (
        l.sem(n) for n in ("log_ok", "gap_ok", "th_ok", "cw_ok", "pcw_ok", "cwb_ok", "part_ok", "addf_ok", "chain"))
    last_ok, out_ok, stored = (l.sem(n) for n in ("last_ok", "out_ok", "stored"))
    GEL_CREDIT, Y_CREDIT, PART_CREDIT, ADD_CREDIT, CWB_CREDIT = RING, RING, 2, 2, 1
    LINKS = 10

    def wrap(r, s):
        return (r + 1, s - NS) if s >= NS else (r, s)

    def split_step(s):
        return s // K, s % K // (FF // P), s % (FF // P)

    LOGITS, RANKS, TANH, WEIGHTS = [-14], [-13, -11, -10, -9], [-8], [-7]
    SPREAD = [-6 + 3 * e for e in range(NE)]
    KEEP = [-4 + 3 * e for e in range(NE)]

    def due(steps, s):
        return [(c, x) for c in range(NCH + 1) for x, at in enumerate(steps) if K * c + at == s]

    def before(steps):
        return [x for x, at in enumerate(steps) if at < 0]

    with nc.Block() as block:

        @block.tensor
        def _(pe):
            def up(r, s):
                r, s = wrap(r, s)
                c, e, q = split_step(s)
                if s % K == 0:
                    pe.wait_ge(cur_ok, NCH * r + c + 1)
                pe.wait_ge(gel_ok, NS * r + s - RING + 1 + GEL_CREDIT)
                f = slice(q * P, (q + 1) * P)
                h = hid[s % RING][:, :]
                nc.tensor.matmul(h, m.w1_hi[:, e, f], cur_hi[:, c, :], start=True, stop=False)
                nc.tensor.matmul(h, m.w1_hi[:, e, f], cur_lo[:, c, :], start=False, stop=False)
                nc.tensor.matmul(h, m.w1_lo[:, e, f], cur_hi[:, c, :], start=False, stop=True).then_inc(hid_ok, 1)

            def down(r, s):
                c, e, q = split_step(s)
                n = NE * (NCH * r + c) + e
                if q == 0:
                    pe.wait_ge(part_ok, n - 1 + PART_CREDIT)
                pe.wait_ge(lo_ok, NS * r + s + 1)
                o, x, first, last = y[e % 2][:, :], e * (FF // P) + q, q == 0, q == FF // P - 1
                nc.tensor.matmul(o, m.w2_hi[:, x, :], gel_hi[s % RING][:, :], start=first, stop=False)
                nc.tensor.matmul(o, m.w2_lo[:, x, :], gel_hi[s % RING][:, :], start=False, stop=False)
                nc.tensor.matmul(o, m.w2_hi[:, x, :], gel_lo[s % RING][:, :], start=False, stop=last).then_inc(y_ok, 1)

            def logits(r, c):
                if not isinstance(r, int):
                    pe.wait_ge(cur_ok, NCH * r + c + 1)
                for i in range(TPC):
                    mm = nc.tensor.matmul(plog[:, i * NE:(i + 1) * NE], m.cur[:, c % NCH, i * P:(i + 1) * P],
                                          m.wg[:, r + c // NCH, :], start=True, stop=True)
                mm.then_inc(log_ok, 1)

            def spread(r, c, e):
                n = NE * (NCH * r + c) + e
                pe.wait_ge(cw_ok, NCH * r + c + 1)
                pe.wait_ge(cwb_ok, n + CWB_CREDIT)
                for i in range(TPC):
                    mm = nc.tensor.transpose(pcw[:, i * P:(i + 1) * P], cw[:, i, e:e + 1].broadcast_to([P, P]),
                                             m.ident[:, :])
                mm.then_inc(pcw_ok, 1)

            nc.tensor.sem_inc(gel_ok, GEL_CREDIT)
            nc.tensor.sem_inc(y_ok, Y_CREDIT)
            nc.tensor.sem_inc(part_ok, PART_CREDIT)
            nc.tensor.sem_inc(add_ok, ADD_CREDIT)
            nc.tensor.sem_inc(cwb_ok, CWB_CREDIT)
            logits(0, 0)
            for s in range(AHEAD):
                up(0, s)
            for e in before(SPREAD):
                spread(0, 0, e)
            with pe.Fori(0, R) as r:
                for s in range(NS):
                    up(r, s + AHEAD)
                    for c, _ in due(LOGITS, s):
                        logits(r, c)
                    for c, e in due(SPREAD, s):
                        spread(r, c, e)
                    down(r, s)
            for c in range(NCH):
                pe.wait_ge(add_ok, NE * (NCH * (R - 1) + c + 1) + ADD_CREDIT)
                if c == 0:
                    pe.wait_ge(gel_ok, NS * R + 1 + GEL_CREDIT)
                for i in range(TPC):
                    mm = nc.tensor.matmul(hid[(c + 3) % RING][:, i * P:(i + 1) * P], m.cur[:, c, i * P:(i + 1) * P],
                                          m.gbd[:, c // 2, :], start=True, stop=True)
                mm.then_inc(last_ok, 1)

        @block.scalar
        def _(act):
            def gelu(r, s):
                r, s = wrap(r, s)
                c, e, q = split_step(s)
                act.wait_ge(hid_ok, NS * r + s + 1)
                act.wait_ge(y_ok, NS * r + s - RING + 1 + Y_CREDIT)
                bias = m.b1[:, e, q:q + 1]
                nc.scalar.activation(gel[s % RING][:, :], hid[s % RING][:, :], ACT.Gelu_apprx_tanh, bias=bias)
                nc.scalar.activation(gel_hi[s % RING][:, :], hid[s % RING][:, :], ACT.Gelu_apprx_tanh,
                                     bias=bias).then_inc(gel_ok, 1)

            def keep(r, c, e):
                n = NE * (NCH * r + c) + e
                act.wait_ge(pcw_ok, n + 1)
                nc.scalar.activation(cwb[:, e, :], pcw[:, :], ACT.Copy).then_inc(cwb_ok, 1)

            def tanh(r, c):
                act.wait_ge(gap_ok, NCH * r + c + 1)
                nc.scalar.activation(th[:, :, :], gap[:, :, :], ACT.Tanh).then_inc(th_ok, 1)

            nc.scalar.activation(cur_hi[:, 0, :], m.cur[:, 0, :], ACT.Copy).then_inc(hi_ok, 1)
            gelu(0, 0)
            tanh(0, 0)
            for e in before(KEEP):
                keep(0, 0, e)
            with act.Fori(0, R) as r:
                for s in range(NS):
                    gelu(r, s + 1)
                    for c, _ in due(TANH, s):
                        tanh(r, c)
                    for c, e in due(KEEP, s):
                        keep(r, c, e)

        @block.vector
        def _(v):
            def low(r, s):
                r, s = wrap(r, s)
                v.wait_ge(gel_ok, NS * r + s + 1 + GEL_CREDIT)
                nc.vector.tensor_tensor(gel_lo[s % RING][:, :], gel[s % RING][:, :], gel_hi[s % RING][:, :],
                                        ALU.subtract).then_inc(lo_ok, 1)

            def linker(r, c, at):
                at = [at]

                def link(ins):
                    at[0] += 1
                    ins.then_inc(chain, 1)
                    v.wait_ge(chain, LINKS * (NCH * r + c) + at[0])
                return link

            def ranks(r, c, stage):
                link = linker(r, c, [0, 3, 5, 7][stage])
                if stage == 0:
                    v.wait_ge(log_ok, NCH * r + c + 1)
                    link(nc.vector.tensor_tensor(log[:, :, :], plog[:, 0:TPC * NE].rearrange("p (t e) -> p t e", e=NE),
                                                 m.bg[:, r + c // NCH, :, :].broadcast_to([P, TPC, NE]), ALU.add))
                    other = log[:, :, :].rearrange("p t (e j) -> p t e j", e=1).broadcast_to([P, TPC, NE, NE])
                    own = log[:, :, :].rearrange("p t (e j) -> p t e j", j=1).broadcast_to([P, TPC, NE, NE])
                    link(nc.vector.tensor_tensor(ge[:, :, :, :], other, own, ALU.is_ge))
                    link(nc.vector.tensor_tensor(gt[:, :, :, :], other, own, ALU.is_gt))
                if stage == 1:
                    tri = [m.tri[:, i:i + 1, :, :].broadcast_to([P, TPC, NE, NE]) for i in range(2)]
                    nc.vector.tensor_tensor(ge[:, :, :, :], ge[:, :, :, :], tri[0], ALU.mult)
                    link(nc.vector.tensor_tensor(gt[:, :, :, :], gt[:, :, :, :], tri[1], ALU.mult))
                    link(nc.vector.tensor_tensor(ge[:, :, :, :], ge[:, :, :, :], gt[:, :, :, :], ALU.add))
                if stage == 2:
                    link(nc.vector.tensor_reduce(rank[:, :, :], ge[:, :, :, :], AX.X, ALU.add))
                    nc.vector.tensor_scalar(half[:, :, :], rank[:, :, :], 1.5, 0.5, ALU.is_lt, ALU.mult)
                    link(nc.vector.tensor_scalar(hdiff[:, :, :], rank[:, :, :], 0.5, None, ALU.is_lt))
                if stage == 3:
                    link(nc.vector.tensor_tensor(hdiff[:, :, :], hdiff[:, :, :], half[:, :, :], ALU.subtract))
                    link(nc.vector.tensor_tensor(dl[:, :, :], hdiff[:, :, :], log[:, :, :], ALU.mult))
                    nc.vector.tensor_reduce(gap[:, :, :], dl[:, :, :], AX.X, ALU.add).then_inc(gap_ok, 1)

            def weights(r, c):
                link = linker(r, c, LINKS - 1)
                v.wait_ge(th_ok, NCH * r + c + 1)
                link(nc.vector.tensor_tensor(cw[:, :, :], hdiff[:, :, :], th[:, :, :].broadcast_to([P, TPC, NE]),
                                             ALU.mult))
                nc.vector.tensor_tensor(cw[:, :, :], cw[:, :, :], half[:, :, :], ALU.add).then_inc(cw_ok, 1)

            def combine(r, c, e):
                n = NE * (NCH * r + c) + e
                v.wait_ge(y_ok, NS * r + K * c + (e + 1) * (FF // P) + Y_CREDIT)
                v.wait_ge(cwb_ok, n + 1 + CWB_CREDIT)
                v.wait_ge(add_ok, n - 1 + ADD_CREDIT)
                nc.vector.scalar_tensor_tensor(out=part[:, e % 2, :], in0=y[e % 2][:, :], scalar=m.b2[:, e:e + 1],
                                               in1=cwb[:, e, :], op0=ALU.add, op1=ALU.mult).then_inc(part_ok, 1)

            v.wait_ge(hi_ok, 1)
            nc.vector.tensor_tensor(cur_lo[:, 0, :], m.cur[:, 0, :], cur_hi[:, 0, :], ALU.subtract).then_inc(cur_ok, 1)
            for stage in range(len(RANKS)):
                ranks(0, 0, stage)
            low(0, 0)
            weights(0, 0)
            with v.Fori(0, R) as r:
                for s in range(NS):
                    low(r, s + 1)
                    for c, stage in due(RANKS, s):
                        ranks(r, c, stage)
                    for c, _ in due(WEIGHTS, s):
                        weights(r, c)
                    if s % (FF // P) == FF // P - 1:
                        combine(r, *split_step(s)[:2])
            for c in range(NCH):
                v.wait_ge(last_ok, c + 1)
                xs = m.x[:, TPC * c:TPC * (c + 1), :]
                nc.vector.tensor_tensor(xs, xs, hid[(c + 3) % RING][:, :].rearrange("p (t e) -> p t e", e=E),
                                        ALU.add).then_inc(out_ok, 1)

        @block.gpsimd
        def _(pool):
            def parts(c, n):
                nc.gpsimd.tensor_copy(cur_hi[:, c, :], m.cur[:, c, :]).then_inc(hi_ok, 1)
                pool.wait_ge(hi_ok, n + 1)
                nc.gpsimd.tensor_tensor(cur_lo[:, c, :], m.cur[:, c, :], cur_hi[:, c, :],
                                        ALU.subtract).then_inc(cur_ok, 1)

            pool.wait_ge(cur_ok, 1)
            for c in range(1, NCH):
                parts(c, c)
            with pool.Fori(0, R) as r:
                for c in range(NCH):
                    for e in range(NE):
                        n = NE * (NCH * r + c) + e
                        pool.wait_ge(part_ok, n + 1 + PART_CREDIT)
                        pool.wait_ge(add_ok, n + ADD_CREDIT)
                        nc.gpsimd.tensor_tensor(m.cur[:, c, :], m.cur[:, c, :], part[:, e % 2, :],
                                                ALU.add).then_inc(add_ok, 1)
                    pool.wait_ge(hi_ok, NCH)
                    pool.wait_ge(add_ok, n + 1 + ADD_CREDIT)
                    parts(c, NCH * (r + 1) + c)

        @block.sync
        def _(sp):
            for c in range(NCH):
                sp.wait_ge(out_ok, c + 1)
                sp.dma_start(m.out.rearrange("b (t p) e -> p (b t) e", p=P)[:, TPC * c:TPC * (c + 1), :],
                             m.x[:, TPC * c:TPC * (c + 1), :]).then_inc(stored, 16)
            sp.wait_ge(stored, 16 * NCH)


def constants():
    def bf16_bits(a):
        return np.ascontiguousarray(a, np.float32).view(np.uint32) >> 16

    inv = 1.0 / 10000.0 ** (np.arange(0, D, 2, dtype=np.float32) / D)
    ang = np.outer(np.arange(T, dtype=np.float32), inv)
    pair = np.arange(P) % (HG * D) // HG // 2
    page = np.arange(T) // PAGE
    k_rows = np.zeros((P - ROW_ZERO, T), np.float32)
    k_rows[ROW_PAGE - ROW_ZERO:ROW_PAGE - ROW_ZERO + NPAGE] = page[None, :] == np.arange(NPAGE)[:, None]
    k_rows[ROW_MAX - ROW_ZERO:] = 1.0
    q_rows = np.zeros((ROW_MAX - ROW_ZERO, T), np.float32)
    q_rows[ROW_PAGE - ROW_ZERO:ROW_PAGE - ROW_ZERO + NPAGE] = np.where(page[None, :] < np.arange(NPAGE)[:, None], MASKED, 0.0)
    j, e = np.arange(NE)[None, :], np.arange(NE)[:, None]
    return {
        "cos": np.ascontiguousarray(np.cos(ang).T[pair]),
        "sin": np.ascontiguousarray(np.sin(ang).T[pair]),
        "ident": np.eye(P, dtype=np.float32),
        "k_rows": bf16_bits(k_rows).astype(np.uint16),
        "q_rows": bf16_bits(q_rows).astype(np.uint16),
        "tri": np.broadcast_to(np.stack([j < e, j > e]).astype(np.float32), (P, 2, NE, NE)).copy(),
    }


_INS = {
    "x": "L0_attn_x", "wq": "L0_attn_wq", "w_down": "L0_attn_w_down", "wk_up": "L0_attn_wk_up",
    "wv_up": "L0_attn_wv_up", "wo": "L0_attn_wo", "Wg": "L0_ffn_Wg", "bg": "L0_ffn_bg", "W1": "L0_ffn_W1",
    "b1": "L0_ffn_b1", "W2": "L0_ffn_W2", "b2": "L0_ffn_b2", "c": "L0_c", "wmod": "L0_wmod",
}


def kernel(**inputs):
    import concourse.bacc as bacc
    from concourse.bass_utils import run_bass_kernel_spmd

    nc = bacc.Bacc("TRN2", target_bir_lowering=False, num_devices=1)
    arrays, dram = {}, {}
    given = {name: np.ascontiguousarray(inputs[full]) for name, full in _INS.items()}
    for name in ("wq", "wk_up"):
        a = given[name]
        given[name] = np.ascontiguousarray(a.reshape(-1, NG, HG, D).transpose(0, 1, 3, 2).reshape(a.shape))
    given["c"] = np.ascontiguousarray(given["c"].T)
    given["Wg"] = np.ascontiguousarray(given["Wg"].transpose(1, 0, 2))
    given["bg"] = np.ascontiguousarray(np.broadcast_to(given["bg"][None, :, None, :], (P, R, 1, NE)))
    given["b1"] = np.ascontiguousarray(given["b1"].reshape(NE, FF // P, P).transpose(2, 0, 1))
    given["b2"] = np.ascontiguousarray(given["b2"].T)
    for name, a in {**given, **constants()}.items():
        arrays[f"in_{name}"] = a
        dram[name] = nc.dram_tensor(f"in_{name}", a.shape, mybir.dt.from_np(a.dtype), kind="ExternalInput").ap()
    out = nc.dram_tensor("out", (B, T, E), F32, kind="ExternalOutput").ap()
    adaln_block(nc, dram, out)
    return run_bass_kernel_spmd(nc, [arrays], core_ids=[0]).results[0]["out"]
```
